# Optimizing a Trainium2 kernel written in Bass

```python
import numpy as np
import jax
import jax.numpy as jnp

def _softmax(x, axis=-1):
    return jax.nn.softmax(x, axis=axis)

def _gelu(x):
    return jax.nn.gelu(x, approximate=True)

def _silu(x):
    return jax.nn.silu(x)

def _sigmoid(x):
    return jax.nn.sigmoid(x)

def _layernorm(x, axis=-1, eps=1e-05):
    m = jnp.mean(x, axis=axis, keepdims=True)
    v = jnp.var(x, axis=axis, keepdims=True)
    return (x - m) / jnp.sqrt(v + eps)

def _scatter_add(tgt, idx, src, axis=0):
    return tgt.at[idx].add(src)

def _segment_sum(src, seg, n):
    return jax.ops.segment_sum(src, seg, n)
kernel_name = 'mk_adaln_d1_jaxref_r8_ebda3e'

def setup_inputs(seed: int=0):
    np.random.seed(seed)
    _w = jnp.asarray

    def _L0_attn_setup():
        import jax, jax.numpy as jnp
        import numpy as np
        import math
        N_HEADS, D_HEAD, D_MODEL = (16, 64, 128)
        B, S = (4, 256)
        NEG_MASK = -100000.0
        key = jax.random.key(seed)
        ks = jax.random.split(key, 9)
        bound = math.sqrt(6.0 / (D_MODEL + D_HEAD))

        def w(k):
            return jax.random.uniform(k, (N_HEADS, D_MODEL, D_HEAD), jnp.float32, -bound, bound)
        return {'x': jax.random.normal(ks[0], (B, S, D_MODEL), jnp.float32), 'Q_w': w(ks[1]), 'Q_b': jnp.zeros((N_HEADS, D_HEAD), jnp.float32), 'K_w': w(ks[2]), 'K_b': jnp.zeros((N_HEADS, D_HEAD), jnp.float32), 'V_w': w(ks[3]), 'V_b': jnp.zeros((N_HEADS, D_HEAD), jnp.float32), 'O_w': jax.random.uniform(ks[4], (N_HEADS, D_HEAD, D_MODEL), jnp.float32, -bound, bound), 'O_b': jnp.zeros((D_MODEL,), jnp.float32)}
    _L0_attn_in = _L0_attn_setup()

    def _L0_ffn_setup():
        import jax, jax.numpy as jnp
        import numpy as np
        B, S, H, F, E, R, TOPK = (4, 256, 128, 512, 4, 4, 2)

        def _more_forward(x, Wg, bg, W1, b1, W2, b2):
            b, s, h = x.shape
            cur = x
            for r in range(R):
                flat = cur.reshape(-1, h)
                logits = flat @ Wg[r] + bg[r]
                vals, idx = jax.lax.top_k(logits, TOPK)
                w = jax.nn.softmax(vals, axis=-1)
                cw = jnp.sum(jax.nn.one_hot(idx, E, dtype=flat.dtype) * w[..., None], axis=1)
                hmid = jax.nn.gelu(jnp.einsum('nh,ehf->enf', flat, W1) + b1[:, None, :])
                y = jnp.einsum('enf,efh->enh', hmid, W2) + b2[:, None, :]
                out = jnp.einsum('ne,enh->nh', cw, y)
                cur = cur + out.reshape(b, s, h)
            return cur
        key = jax.random.key(seed)
        ks = jax.random.split(key, 8)
        scale = 0.02
        return {'x': jax.random.normal(ks[0], (B, S, H), dtype=jnp.float32), 'Wg': jax.random.normal(ks[1], (R, H, E), dtype=jnp.float32) * scale, 'bg': jnp.zeros((R, E), dtype=jnp.float32), 'W1': jax.random.normal(ks[2], (E, H, F), dtype=jnp.float32) * scale, 'b1': jnp.zeros((E, F), dtype=jnp.float32), 'W2': jax.random.normal(ks[3], (E, F, H), dtype=jnp.float32) * scale, 'b2': jnp.zeros((E, H), dtype=jnp.float32)}
    _L0_ffn_in = _L0_ffn_setup()
    _L0_c = _w((lambda *s: np.random.randn(*s).astype(np.float32) * 0.05)(8, 128))
    _L0_wmod = _w((lambda *s: np.random.randn(*s).astype(np.float32) * 0.05)(128, 6 * 128) * 128 ** (-0.5))
    _d = {'L0_attn_x': _L0_attn_in['x'], 'L0_attn_Q_w': _L0_attn_in['Q_w'], 'L0_attn_Q_b': _L0_attn_in['Q_b'], 'L0_attn_K_w': _L0_attn_in['K_w'], 'L0_attn_K_b': _L0_attn_in['K_b'], 'L0_attn_V_w': _L0_attn_in['V_w'], 'L0_attn_V_b': _L0_attn_in['V_b'], 'L0_attn_O_w': _L0_attn_in['O_w'], 'L0_attn_O_b': _L0_attn_in['O_b'], 'L0_ffn_Wg': _L0_ffn_in['Wg'], 'L0_ffn_bg': _L0_ffn_in['bg'], 'L0_ffn_W1': _L0_ffn_in['W1'], 'L0_ffn_b1': _L0_ffn_in['b1'], 'L0_ffn_W2': _L0_ffn_in['W2'], 'L0_ffn_b2': _L0_ffn_in['b2'], 'L0_c': _L0_c, 'L0_wmod': _L0_wmod}
    _x0 = _d['L0_attn_x']
    _d['L0_attn_x'] = jax.random.normal(jax.random.fold_in(jax.random.key(seed), 1), (8, 512, 128), dtype=_x0.dtype)
    del _x0
    return _d

def reference(L0_attn_x, L0_attn_Q_w, L0_attn_Q_b, L0_attn_K_w, L0_attn_K_b, L0_attn_V_w, L0_attn_V_b, L0_attn_O_w, L0_attn_O_b, L0_ffn_Wg, L0_ffn_bg, L0_ffn_W1, L0_ffn_b1, L0_ffn_W2, L0_ffn_b2, L0_c, L0_wmod):

    def _L0_attn_ref(x, Q_w, Q_b, K_w, K_b, V_w, V_b, O_w, O_b):
        import jax, jax.numpy as jnp
        import numpy as np
        import math
        N_HEADS, D_HEAD, D_MODEL = (16, 64, 128)
        B, S = (4, 256)
        NEG_MASK = -100000.0
        q = jnp.einsum('bpm,hmd->bphd', x, Q_w) + Q_b
        k = jnp.einsum('bpm,hmd->bphd', x, K_w) + K_b
        v = jnp.einsum('bpm,hmd->bphd', x, V_w) + V_b
        logits = jnp.einsum('bqhd,bkhd->bhqk', q, k) / math.sqrt(D_HEAD)
        s = logits.shape[-1]
        causal = jnp.triu(jnp.ones((s, s), dtype=bool), k=1)
        logits = jnp.where(causal, NEG_MASK, logits)
        scores = jax.nn.softmax(logits, axis=-1)
        attn = jnp.einsum('bhqk,bkhd->bqhd', scores, v)
        return jnp.einsum('bqhd,hdm->bqm', attn, O_w) + O_b

    def _L0_ffn_ref(x, Wg, bg, W1, b1, W2, b2):
        import jax, jax.numpy as jnp
        import numpy as np
        B, S, H, F, E, R, TOPK = (4, 256, 128, 512, 4, 4, 2)

        def _more_forward(x, Wg, bg, W1, b1, W2, b2):
            b, s, h = x.shape
            cur = x
            for r in range(R):
                flat = cur.reshape(-1, h)
                logits = flat @ Wg[r] + bg[r]
                vals, idx = jax.lax.top_k(logits, TOPK)
                w = jax.nn.softmax(vals, axis=-1)
                cw = jnp.sum(jax.nn.one_hot(idx, E, dtype=flat.dtype) * w[..., None], axis=1)
                hmid = jax.nn.gelu(jnp.einsum('nh,ehf->enf', flat, W1) + b1[:, None, :])
                y = jnp.einsum('enf,efh->enh', hmid, W2) + b2[:, None, :]
                out = jnp.einsum('ne,enh->nh', cw, y)
                cur = cur + out.reshape(b, s, h)
            return cur
        return _more_forward(x, Wg, bg, W1, b1, W2, b2)
    x = L0_attn_x
    mod = (_silu(L0_c) @ L0_wmod).reshape(L0_c.shape[0], 6, 1, -1)
    sa, ca, ga, sb, cb, gb = (mod[:, 0], mod[:, 1], mod[:, 2], mod[:, 3], mod[:, 4], mod[:, 5])
    ga = (2 * (ga >= 0) - 1) * jnp.maximum(jnp.abs(ga), 0.25)
    gb = (2 * (gb >= 0) - 1) * jnp.maximum(jnp.abs(gb), 0.25)
    h = _layernorm(x, axis=-1) * (1 + ca) + sa
    x = x + ga * _L0_attn_ref(h, L0_attn_Q_w, L0_attn_Q_b, L0_attn_K_w, L0_attn_K_b, L0_attn_V_w, L0_attn_V_b, L0_attn_O_w, L0_attn_O_b)
    h = _layernorm(x, axis=-1) * (1 + cb) + sb
    x = x + gb * _L0_ffn_ref(h, L0_ffn_Wg, L0_ffn_bg, L0_ffn_W1, L0_ffn_b1, L0_ffn_W2, L0_ffn_b2)
    return x

_drawn_inputs = setup_inputs


def setup_inputs(seed=0):
    import zlib

    import numpy as np

    out = dict(_drawn_inputs(seed))
    spreads = {'L0_attn_Q_b': (0.0, 0.392),
     'L0_attn_K_b': (0.0, 0.8),
     'L0_attn_V_b': (0.0, 0.1),
     'L0_attn_O_b': (0.0, 0.337),
     'L0_ffn_bg': (0.0, 0.501),
     'L0_ffn_b1': (0.0, 0.644),
     'L0_ffn_b2': (0.0, 0.1)}
    factors = {}
    for name, (base, spread) in spreads.items():
        noise = np.random.default_rng([zlib.crc32(name.encode()), seed]).standard_normal(out[name].shape)
        drawn = base * np.exp(spread * noise) if base else spread * noise
        out[name] = jnp.asarray(drawn.astype(out[name].dtype))
    for name, factor in factors.items():
        out[name] = (out[name] * factor).astype(out[name].dtype)
    return out
```

```python
from contextlib import ExitStack

import concourse.bass as bass
from concourse import mybir
from concourse.alu_op_type import AluOpType as ALU

ACT = mybir.ActivationFunctionType
F32 = mybir.dt.float32
F32R = mybir.dt.float32r
AX_X = mybir.AxisListType.X

P = 128
EPS = 1e-5
NEG = -1.0e30
BIG = 3.0e38




def adaln_block(nc, ins, out):
    x_d, qw_d, qb_d, kw_d, kb_d, vw_d, vb_d, ow_d, ob_d, wg_d, bg_d, w1_d, b1_d, w2_d, b2_d, c_d, wmod_d = ins
    B, S, D = x_d.shape
    H, _, DH = qw_d.shape
    R, _, E = wg_d.shape
    F = w1_d.shape[2]
    TILES = S // P
    PAIRS = H // 2
    FC = F // P
    SCALE = float(DH) ** -0.5
    assert D == P and DH == 64 and S == 512 and TILES == 4 and H == 16 and E == 4

    P_OFF = [P * (i * (i + 1) // 2) for i in range(TILES + 1)]
    P_COLS = P_OFF[TILES]
    PT_OFF = [0, 512, 1152, 896]
    PT_DATA3 = 1024
    PT_COLS = 1408
    CHUNKS = [
        ([(i, 0) for i in range(4)], 0),
        ([(i, 1) for i in range(1, 4)], 512),
        ([(3, 3), (2, 2), (3, 2)], PT_DATA3),
    ]

    ITEMS = [[] for _ in range(H)]
    for pair in range(2, PAIRS):
        ITEMS[2 * pair - 4].append(("q", pair, 0))
        ITEMS[2 * pair - 3].append(("k", pair, 0))
    for step, tile, rel in [(0, 3, 0), (3, 4, 0), (5, 5, 0), (7, 6, 0), (8, 7, 0), (14, 0, 1), (15, 1, 1), (15, 2, 1)]:
        ITEMS[step].append(("v", tile, rel))
    ITEMS[9].append(("h2", 0, -1))
    ITEMS[11].append(("h", 0, 1))
    ITEMS[13] += [("q", 0, 1), ("k", 0, 1)]
    ITEMS[14].insert(0, ("q", 1, 1))
    ITEMS[15].insert(0, ("k", 1, 1))
    FLAT = [(step, item) for step in range(H) for item in ITEMS[step]]
    assert len(FLAT) % 2 == 0

    def there(b):
        return not isinstance(b, int) or 0 <= b < B

    with ExitStack() as whole:
        def sb(ctx, name, shape, dt=F32):
            return ctx.enter_context(nc.sbuf_tensor(name, shape, dt))

        def sem(name):
            return whole.enter_context(nc.semaphore(name))

        x_sb = sb(whole, "x_sb", [P, B * TILES * D])
        cur_all = sb(whole, "cur_all", [P, B * S])
        w1_raw = sb(whole, "w1_raw", [P, E * F])
        w2_raw = sb(whole, "w2_raw", [P, E * FC * D])
        ident = sb(whole, "ident", [P, P])
        modT = sb(whole, "modT", [P, 6, B])
        biasT = sb(whole, "biasT", [P, 40])
        wg_sb = sb(whole, "wg_sb", [P, R * E])
        bg_sb = sb(whole, "bg_sb", [P, R, TILES, E])
        NB1 = E * FC
        QB, KB, B1, B2, OB = 0, PAIRS, 2 * PAIRS, 2 * PAIRS + NB1, 2 * PAIRS + NB1 + E
        NROWS = OB + 1

        ps = [whole.enter_context(nc.psum_tensor(f"bank{i}", [P, 512], F32)) for i in range(8)]

        dve_waited = sem("dve_waited")
        pool_waited = sem("pool_waited")

        ld_c = sem("ld_c")
        ld_bias = sem("ld_bias")
        ld_wmod = sem("ld_wmod")
        ld_x = [sem(f"ld_x{i}") for i in range(2)]
        ld_w = sem("ld_w")
        ld_ffn = sem("ld_ffn")

        with ExitStack() as ctx:
            w_names = ["wq", "wk", "wv", "wo"]
            w_hi = {n: sb(ctx, n + "_hi", [P, H * DH], F32R) for n in w_names}
            w_lo = {n: sb(ctx, n + "_lo", [P, H * DH], F32R) for n in w_names}
            v_hl = [sb(ctx, f"v_hl{i}", [P, TILES, H // 2, 2 * DH], F32R) for i in range(2)]
            prob = sb(ctx, "prob", [P, 4, P_COLS])
            neg_s = sb(ctx, "neg_s", [P, P_COLS])
            pt_hi = [sb(ctx, f"pt_hi{i}", [P, PT_COLS], F32R) for i in range(2)]
            pt_lo = [sb(ctx, f"pt_lo{i}", [P, PT_COLS], F32R) for i in range(2)]
            q_hi = [sb(ctx, f"q_hi{i}", [P, S], F32R) for i in range(2)]
            q_lo = [sb(ctx, f"q_lo{i}", [P, S], F32R) for i in range(2)]
            k_hi = [sb(ctx, f"k_hi{i}", [P, S], F32R) for i in range(2)]
            k_lo = [sb(ctx, f"k_lo{i}", [P, S], F32R) for i in range(2)]
            h_f = sb(ctx, "h_f", [P, S])
            h_hi = sb(ctx, "h_hi", [P, S], F32R)
            h_lo = sb(ctx, "h_lo", [P, S], F32R)
            norm1 = sb(ctx, "norm1", [P, TILES * D])
            norm2 = sb(ctx, "norm2", [P, TILES * D])
            gated = sb(ctx, "gated", [P, S])
            att = sb(ctx, "att", [P, S])
            att_hi = [sb(ctx, f"att_hi{i}", [P, S], F32R) for i in range(2)]
            att_lo = [sb(ctx, f"att_lo{i}", [P, S], F32R) for i in range(2)]
            att_small = sb(ctx, "att_small", [DH, S])
            mask = sb(ctx, "mask", [P, S])
            negmax = sb(ctx, "negmax", [P, TILES])
            sums = sb(ctx, "sums", [P, 4, TILES])
            rinv = sb(ctx, "rinv", [P, 4, TILES])
            bn1 = sb(ctx, "bn1", [P, TILES, 6])
            bn2 = sb(ctx, "bn2", [P, TILES, 6])
            mv1 = sb(ctx, "mv1", [P, TILES, 2])
            mv2 = sb(ctx, "mv2", [P, TILES, 2])
            ve1 = sb(ctx, "ve1", [P, TILES])
            ve2 = sb(ctx, "ve2", [P, TILES])
            rstd1 = sb(ctx, "rstd1", [P, TILES])
            rstd2 = sb(ctx, "rstd2", [P, TILES])
            minus_half = sb(ctx, "minus_half", [P, TILES])
            vbT = sb(ctx, "vbT", [DH, H])
            raw = {n: prob[:, i, 0:H * DH] for i, n in enumerate(w_names)}
            wmod_raw = cur_all[:, 0:6 * D]
            c_sb = cur_all[0:B, 1024:1024 + D]
            c_act = cur_all[0:B, 1152:1152 + D]
            c_tanh = cur_all[0:B, 1280:1280 + D]
            siluT = cur_all[:, 1408:1408 + B]
            rows = cur_all[0:NROWS, 1536:1536 + P]
            vb_rows = cur_all[0:H, 1664:1664 + DH]
            ga_pos = cur_all[:, 1792:1792 + 2 * B]
            ga_neg = cur_all[:, 1856:1856 + 2 * B]

            su_const = sem("su_const")
            su_tanh = sem("su_tanh")
            su_dve = sem("su_dve")
            su_pe = sem("su_pe")
            su_whi = sem("su_whi")
            su_wlo = sem("su_wlo")
            pe_item = {n: sem("pe_" + n) for n in ("q", "k", "v", "h", "h2")}
            pe_s = sem("pe_s")
            pe_t = sem("pe_t")
            pe_pv = sem("pe_pv")
            pe_o = sem("pe_o")
            pe_yt = sem("pe_yt")
            act_item = {n: sem("act_" + n) for n in ("q", "k", "v", "h")}
            act_exp = sem("act_exp")
            act_pt = sem("act_pt")
            act_small = sem("act_small")
            dve_item = {n: sem("dve_" + n) for n in ("q", "k", "v", "h", "h2")}
            dve_min = sem("dve_min")
            dve_pt = sem("dve_pt")
            dve_rinv = sem("dve_rinv")
            dve_att = sem("dve_att")
            dve_y = sem("dve_y")
            dve_x1 = sem("dve_x1")
            dve_bn1 = sem("dve_bn1")
            dve_bn2 = sem("dve_bn2")
            dve_ve1 = sem("dve_ve1")
            dve_ve2 = sem("dve_ve2")
            dve_norm1 = sem("dve_norm1")
            dve_norm2 = sem("dve_norm2")
            pool_hlo = sem("pool_hlo")
            pool_prob = sem("pool_prob")
            pool_ahi = sem("pool_ahi")
            pool_alo = sem("pool_alo")
            pool_rstd1 = sem("pool_rstd1")
            pool_rstd2 = sem("pool_rstd2")

            def after(eng, s, n):
                if not isinstance(n, int) or n > 0:
                    eng.wait_ge(s, n)

            def nth(kind, index, b):
                per_row = {"q": PAIRS, "k": PAIRS, "v": 2 * TILES, "h": 1, "h2": 1}[kind]
                return b * per_row + index + 1

            def bank_of(n):
                return ps[n % 2]

            def bank_free(eng, n, b):
                back = n - 2
                while True:
                    step, (kind, index, rel) = FLAT[back % len(FLAT)]
                    row = b + rel + (back // len(FLAT))
                    if there(row):
                        break
                    back -= 2
                    if back < -2 * len(FLAT):
                        return
                after(eng, dve_item[kind], nth(kind, index, row))

            first = {}
            for n, (step, item) in enumerate(FLAT):
                first.setdefault(step, n)

            def items(b, u):
                return [(first[u] + i, kind, index, b + rel)
                        for i, (kind, index, rel) in enumerate(ITEMS[u]) if there(b + rel)]

            def scored(b, u):
                return (b, u + 2) if u + 2 < H else (b + 1, u + 2 - H)

            def weighted(b, u):
                return (b, u - 1) if u else (b - 1, H - 1)

            block = ctx.enter_context(nc.Block())

            @block.sync
            def _(sp):
                sp.dma_start(c_sb, c_d).then_inc(ld_c, 16)
                xv = x_d.rearrange("b (t p) d -> p (b t) d", p=P)
                xs = x_sb[:, :].rearrange("p (n d) -> p n d", d=D)
                sp.dma_start(xs[:, 0:TILES, :], xv[:, 0:TILES, :]).then_inc(ld_x[0], 16)
                sp.dma_start(wmod_raw, wmod_d).then_inc(ld_wmod, 16)
                for n, d in (("wq", qw_d), ("wk", kw_d), ("wv", vw_d)):
                    sp.dma_start(raw[n].rearrange("p (h d) -> p h d", d=DH), d.rearrange("h m d -> m h d")).then_inc(ld_w, 16)
                sp.dma_start(raw["wo"].rearrange("p (n m) -> p n m", m=D),
                             ow_d.rearrange("(n two) d m -> (two d) n m", two=2)).then_inc(ld_w, 16)
                sp.dma_start(xs[:, TILES:, :], xv[:, TILES:, :]).then_inc(ld_x[1], 16)
                sp.dma_start(w1_raw[:, :].rearrange("p (e f) -> p e f", e=E), w1_d.rearrange("e h f -> h e f")).then_inc(ld_ffn, 16)
                sp.dma_start(w2_raw[:, :].rearrange("p (e c h) -> p e c h", e=E, c=FC),
                             w2_d.rearrange("e (c p) h -> p e c h", p=P)).then_inc(ld_ffn, 16)
                sp.dma_start(wg_sb[:, :].rearrange("p (r e) -> p r e", r=R), wg_d.rearrange("r h e -> h r e")).then_inc(ld_ffn, 16)
                for t in range(TILES):
                    sp.dma_start(bg_sb[:, :, t, :], bg_d.partition_broadcast(P)).then_inc(ld_ffn, 16)

            @block.tensor
            def _(pe):
                def three(out_ap, lhs_hi, lhs_lo, rhs_hi, rhs_lo, start=True, stop=True):
                    nc.tensor.matmul(out_ap, lhs_hi, rhs_hi, start=start, stop=False)
                    nc.tensor.matmul(out_ap, lhs_hi, rhs_lo, start=False, stop=False)
                    return nc.tensor.matmul(out_ap, lhs_lo, rhs_hi, start=False, stop=stop)

                pe.wait_ge(su_const, 4)
                pe.wait_ge(ld_bias, 16 * 6)
                nc.tensor.transpose(ps[2][:, 0:NROWS], rows, ident[0:NROWS, 0:NROWS])
                nc.tensor.transpose(ps[2][0:DH, 64:64 + H], vb_rows, ident[0:H, 0:H])
                pe.wait_ge(su_dve, 1)
                nc.tensor.transpose(ps[2][:, 128:128 + B], c_act, ident[0:B, 0:B]).then_inc(su_pe, 1)
                pe.wait_ge(su_dve, 2)
                pe.wait_ge(ld_wmod, 16)
                for j in range(6):
                    last = nc.tensor.matmul(ps[3][:, j * B:(j + 1) * B], wmod_raw[:, j * D:(j + 1) * D], siluT, start=True, stop=True)
                last.then_inc(su_pe, 1)

                def item(b, n, kind, index, row):
                    bank_free(pe, n, b)
                    bank = bank_of(n)
                    done = pe_item[kind]
                    if kind in ("q", "k"):
                        if kind == "q" and index == 0:
                            pe.wait_ge(pool_hlo, row + 1)
                            pe.wait_ge(su_wlo, 4)
                        w = slice(index * P, (index + 1) * P)
                        name = "w" + kind
                        three(bank[:, :], w_hi[name][:, w], w_lo[name][:, w], h_hi[:, :], h_lo[:, :]).then_inc(done, 1)
                    if kind == "v":
                        half, t = divmod(index, TILES)
                        tok, cols = slice(t * P, (t + 1) * P), slice(half * 512, (half + 1) * 512)
                        three(bank[:, :], h_hi[:, tok], h_lo[:, tok], w_hi["wv"][:, cols], w_lo["wv"][:, cols]).then_inc(done, 1)
                    if kind in ("h", "h2"):
                        src = norm1 if kind == "h" else norm2
                        pe.wait_ge(dve_norm1 if kind == "h" else dve_norm2, row + 1)
                        for t in range(TILES):
                            tok = slice(t * P, (t + 1) * P)
                            last = nc.tensor.transpose(bank[:, tok], src[:, tok], ident[:, :])
                        last.then_inc(done, 1)

                def scores(b, u):
                    pair, lo = u // 2, DH * (u % 2)
                    half = slice(lo, lo + DH)
                    if u % 2 == 0:
                        after(pe, dve_item["q"], nth("q", pair, b))
                        after(pe, dve_item["k"], nth("k", pair, b))
                    for i in range(TILES):
                        n = (b * H + u) * TILES + i
                        after(pe, dve_min, n - 1)
                        tok, keys = slice(i * P, (i + 1) * P), slice(0, max(256, (i + 1) * P))
                        three(ps[2 + i % 2][:, keys], q_hi[pair % 2][half, tok], q_lo[pair % 2][half, tok],
                              k_hi[pair % 2][half, keys], k_lo[pair % 2][half, keys]).then_inc(pe_s, 1)

                def values(b, u):
                    pair = u // 2
                    if u % (H // 2) == 0:
                        after(pe, dve_item["v"], nth("v", TILES * (u * 2 // H) + TILES - 1, b))
                    after(pe, dve_pt, (b * H + u) * 3 + 3)
                    after(pe, dve_att, b * H + u)
                    for j in (0, 1, 2, 3):
                        width = max(256, S - j * P)
                        stat = v_hl[u * 2 // H][:, j, u % (H // 2), :]
                        cols = slice(PT_OFF[j], PT_OFF[j] + width)
                        for n, part in enumerate((pt_hi, pt_lo)):
                            last = nc.tensor.matmul(ps[6][:, S - width:S], stat, part[u % 2][:, cols],
                                                    start=(j == 0 and n == 0), stop=(j == 3 and n == 1))
                    last.then_inc(pe_pv, 1)

                def turn(b, u):
                    after(pe, pool_prob, b * H + u + 1)
                    for c, (blocks, _) in enumerate(CHUNKS):
                        n = (b * H + u) * 3 + c
                        after(pe, dve_pt, n - 1)
                        bank = ps[4 + (u * 3 + c) % 2]
                        for z, (i, j) in enumerate(blocks):
                            col = P_OFF[i] + j * P
                            last = nc.tensor.transpose(bank[:, z * P:(z + 1) * P], prob[:, u % 4, col:col + P], ident[:, :])
                        last.then_inc(pe_t, 1)

                def project(b, pair):
                    after(pe, pool_alo, b * PAIRS + pair + 1)
                    if pair == 0:
                        after(pe, dve_x1, b)
                    w = slice(pair * D, (pair + 1) * D)
                    three(ps[7][:, :], w_hi["wo"][:, w], w_lo["wo"][:, w], att_hi[pair % 2][:, :], att_lo[pair % 2][:, :],
                          start=(pair == 0), stop=(pair == PAIRS - 1)).then_inc(pe_o, 1)

                def step(b, u):
                    if u == 4 and there(b - 1):
                        after(pe, dve_y, b)
                        for t in range(TILES):
                            tok = slice(t * P, (t + 1) * P)
                            last = nc.tensor.transpose(ps[7][:, tok], gated[:, tok], ident[:, :])
                        last.then_inc(pe_yt, 1)
                    for n, kind, index, row in items(b, u):
                        item(b, n, kind, index, row)
                    row, head = scored(b, u)
                    if there(row):
                        scores(row, head)
                    row, head = weighted(b, u)
                    if there(row):
                        values(row, head)
                    if there(b):
                        turn(b, u)
                    if u == 2 and there(b - 1):
                        project(b - 1, PAIRS - 1)
                    if u >= 4 and u % 2 == 0 and there(b):
                        project(b, (u - 4) // 2)
                    if u == 0 and there(b - 1):
                        project(b - 1, PAIRS - 2)

                for u in range(8, H):
                    step(-1, u)
                for u in range(H):
                    step(0, u)
                with pe.Fori(1, B - 1) as b:
                    for u in range(H):
                        step(b, u)
                for u in range(H):
                    step(B - 1, u)
                for u in range(10):
                    step(B, u)

            @block.scalar
            def _(act):
                act.dma_start(rows[QB:QB + PAIRS, :], qb_d.rearrange("(n two) d -> n (two d)", two=2)).then_inc(ld_bias, 16)
                act.dma_start(rows[KB:KB + PAIRS, :], kb_d.rearrange("(n two) d -> n (two d)", two=2)).then_inc(ld_bias, 16)
                act.dma_start(rows[B1:B1 + NB1, :], b1_d.rearrange("e (c f) -> (e c) f", f=P)).then_inc(ld_bias, 16)
                act.dma_start(rows[B2:B2 + E, :], b2_d).then_inc(ld_bias, 16)
                act.dma_start(rows[OB:OB + 1, :], ob_d.rearrange("(a m) -> a m", a=1)).then_inc(ld_bias, 16)
                act.dma_start(vb_rows, vb_d).then_inc(ld_bias, 16)
                act.wait_ge(ld_c, 16)
                nc.scalar.activation(c_tanh, c_sb, ACT.Tanh, scale=0.5).then_inc(su_tanh, 1)
                for n, name in enumerate(w_names):
                    act.wait_ge(ld_w, 16 * 4)
                    nc.scalar.copy(w_hi[name][:, :], raw[name]).then_inc(su_whi, 1)

                def item(b, n, kind, index, row):
                    bank = bank_of(n)
                    if kind in ("q", "k"):
                        act.wait_ge(pe_item[kind], nth(kind, index, row))
                        hi, col = (q_hi, QB) if kind == "q" else (k_hi, KB)
                        nc.scalar.activation(hi[index % 2][:, :], bank[:, :], ACT.Identity,
                                             bias=biasT[:, col + index:col + index + 1]).then_inc(act_item[kind], 1)
                    if kind == "v":
                        half, t = divmod(index, TILES)
                        act.wait_ge(pe_item["v"], nth("v", index, row))
                        nc.scalar.copy(v_hl[half][:, t, :, 0:DH],
                                       bank[:, :].rearrange("p (h d) -> p h d", d=DH)).then_inc(act_item["v"], 1)
                    if kind == "h":
                        act.wait_ge(dve_item["h"], row + 1)
                        nc.scalar.copy(h_hi[:, :], h_f[:, :]).then_inc(act_item["h"], 1)

                def exps(b, u):
                    for i in range(TILES):
                        n = (b * H + u) * TILES + i
                        after(act, dve_min, n + 1)
                        if i == 0:
                            after(act, pe_t, (b * H + u - 4) * 3 + 3)
                        w = slice(P_OFF[i], P_OFF[i + 1])
                        nc.scalar.activation(prob[:, u % 4, w], neg_s[:, w], ACT.Exp, scale=-1.0,
                                             bias=negmax[:, i:i + 1], accum_out=sums[:, u % 4, i:i + 1]).then_inc(act_exp, 1)

                def small(b, u):
                    after(act, pe_pv, b * H + u + 1)
                    after(act, dve_att, b * H + u)
                    nc.scalar.copy(att_small[:, :], ps[6][DH:P, :]).then_inc(act_small, 1)

                def turned(b, u):
                    for c, (blocks, dst) in enumerate(CHUNKS):
                        n = (b * H + u) * 3 + c
                        after(act, pe_t, n + 1)
                        if c == 0:
                            after(act, pe_pv, b * H + u - 1)
                        width = len(blocks) * P
                        nc.scalar.copy(pt_hi[u % 2][:, dst:dst + width],
                                       ps[4 + (u * 3 + c) % 2][:, 0:width]).then_inc(act_pt, 1)

                def step(b, u):
                    for n, kind, index, row in items(b, u):
                        item(b, n, kind, index, row)
                    row, head = scored(b, u)
                    if there(row):
                        exps(row, head)
                    row, head = weighted(b, u)
                    if there(row):
                        small(row, head)
                    if there(b):
                        turned(b, u)

                act.wait_ge(su_wlo, 4)
                act.wait_ge(su_dve, 6)
                for u in range(8, H):
                    step(-1, u)
                for u in range(H):
                    step(0, u)
                with act.Fori(1, B - 1) as b:
                    for u in range(H):
                        step(b, u)
                for u in range(H):
                    step(B - 1, u)
                for u in range(10):
                    step(B, u)

            @block.vector
            def _(dve):
                dve.wait_ge(su_tanh, 1)
                nc.vector.scalar_tensor_tensor(out=c_act, in0=c_tanh, scalar=1.0, in1=c_sb, op0=ALU.add, op1=ALU.mult).then_inc(su_dve, 1)
                dve.wait_ge(su_pe, 1)
                nc.vector.tensor_scalar(siluT, ps[2][:, 128:128 + B], 0.5, None, ALU.mult).then_inc(su_dve, 1)
                nc.vector.tensor_copy(biasT[:, 0:NROWS], ps[2][:, 0:NROWS])
                nc.vector.tensor_copy(vbT[:, :], ps[2][0:DH, 64:64 + H])
                dve.wait_ge(su_pe, 2)
                nc.vector.tensor_copy(modT[:, :, :], ps[3][:, 0:6 * B].rearrange("p (j b) -> p j b", b=B)).then_inc(su_dve, 1)
                dve.wait_ge(su_dve, 3)
                g = modT[:, 2:6:3, :]
                ga_pos_v = ga_pos.rearrange("p (j b) -> p j b", b=B)
                ga_neg_v = ga_neg.rearrange("p (j b) -> p j b", b=B)
                nc.vector.tensor_scalar(ga_pos_v, g, 0.0, 2.0, ALU.is_ge, ALU.mult)
                nc.vector.tensor_scalar(ga_neg_v, g, -1.0, None, ALU.mult)
                nc.vector.tensor_scalar(modT[:, 1:5:3, :], modT[:, 1:5:3, :], 1.0, None, ALU.add).then_inc(su_dve, 1)
                dve.wait_ge(su_dve, 4)
                nc.vector.tensor_scalar(ga_pos_v, ga_pos_v, 1.0, None, ALU.subtract)
                nc.vector.tensor_tensor(ga_neg_v, ga_neg_v, g, ALU.max).then_inc(su_dve, 1)
                dve.wait_ge(su_dve, 5)
                nc.vector.scalar_tensor_tensor(out=g, in0=ga_neg_v, scalar=0.25, in1=ga_pos_v, op0=ALU.max, op1=ALU.mult).then_inc(su_dve, 1)
                for n, name in enumerate(w_names):
                    dve.wait_ge(su_whi, n + 1)
                    nc.vector.tensor_tensor(w_lo[name][:, :], raw[name], w_hi[name][:, :].bitcast(F32), ALU.subtract).then_inc(su_wlo, 1)
                dve.wait_ge(su_dve, 6)
                dve.wait_ge(su_const, 7)

                def item(b, n, kind, index, row):
                    bank = bank_of(n)
                    if kind in ("q", "k"):
                        hi, lo, col = (q_hi, q_lo, QB) if kind == "q" else (k_hi, k_lo, KB)
                        dve.wait_ge(act_item[kind], nth(kind, index, row))
                        nc.vector.scalar_tensor_tensor(out=lo[index % 2][:, :], in0=bank[:, :], scalar=biasT[:, col + index:col + index + 1],
                                                       in1=hi[index % 2][:, :].bitcast(F32), op0=ALU.add, op1=ALU.subtract).then_inc(dve_item[kind], 1)
                    if kind == "v":
                        half, t = divmod(index, TILES)
                        dve.wait_ge(act_item["v"], nth("v", index, row))
                        nc.vector.tensor_tensor(v_hl[half][:, t, :, DH:2 * DH], bank[:, :].rearrange("p (h d) -> p h d", d=DH),
                                                v_hl[half][:, t, :, 0:DH].bitcast(F32), ALU.subtract).then_inc(dve_item["v"], 1)
                    if kind == "h":
                        dve.wait_ge(pe_item["h"], row + 1)
                        after(dve, pool_hlo, row)
                        nc.vector.tensor_scalar(h_f[:, :], bank[:, :], modT[:, 1, bass.ds(row, 1)], modT[:, 0, bass.ds(row, 1)],
                                                ALU.mult, ALU.add).then_inc(dve_item["h"], 1)
                    if kind == "h2":
                        dve.wait_ge(pe_item["h2"], row + 1)
                        nc.vector.tensor_scalar(cur_all[:, bass.ds(row * S, S)], bank[:, :], modT[:, 4, bass.ds(row, 1)],
                                                modT[:, 3, bass.ds(row, 1)], ALU.mult, ALU.add).then_inc(dve_item["h2"], 1)

                def minima(b, u):
                    for i in range(TILES):
                        n = (b * H + u) * TILES + i
                        after(dve, pe_s, n + 1)
                        after(dve, act_exp, n + 1 - TILES)
                        dve.sem_inc(dve_waited, 1)
                        w = (i + 1) * P
                        nc.vector.tensor_tensor_reduce(neg_s[:, P_OFF[i]:P_OFF[i + 1]], ps[2 + i % 2][:, 0:w], mask[:, S - w:S],
                                                       -SCALE, BIG, ALU.add, ALU.min, negmax[:, i:i + 1]).then_inc(dve_min, 1)

                def attended(b, u):
                    after(dve, act_small, b * H + u + 1)
                    if u % 2 == 0:
                        after(dve, pool_alo, b * PAIRS + u // 2)
                    r = DH * (u % 2)
                    nc.vector.scalar_tensor_tensor(out=att[r:r + DH, :], in0=ps[6][0:DH, :], scalar=vbT[:, u:u + 1], in1=att_small[:, :],
                                                   op0=ALU.add, op1=ALU.add).then_inc(dve_att, 1)

                def turned(b, u):
                    for c, (blocks, dst) in enumerate(CHUNKS):
                        n = (b * H + u) * 3 + c
                        after(dve, act_pt, n + 1)
                        width = len(blocks) * P
                        nc.vector.tensor_tensor(pt_lo[u % 2][:, dst:dst + width], ps[4 + (u * 3 + c) % 2][:, 0:width],
                                                pt_hi[u % 2][:, dst:dst + width].bitcast(F32), ALU.subtract).then_inc(dve_pt, 1)

                def inverse(b, u):
                    after(dve, act_exp, (b * H + u + 1) * TILES)
                    nc.vector.reciprocal(rinv[:, u % 4, :], sums[:, u % 4, :]).then_inc(dve_rinv, 1)

                def moments(row, stats, mv, ve, s_bn, s_ve):
                    dve.sem_inc(dve_waited, 1)
                    for t in range(TILES):
                        last = nc.vector.bn_stats(stats[:, t, :], x_sb[:, bass.ds(row * S + t * D, D)])
                    last.then_inc(s_bn, 1)
                    after(dve, s_bn, row * 2 + 1)
                    dve.sem_inc(dve_waited, 1)
                    for t in range(TILES):
                        last = nc.vector.bn_aggr(mv[:, t, :], stats[:, t, :])
                    last.then_inc(s_bn, 1)
                    after(dve, s_bn, row * 2 + 2)
                    nc.vector.tensor_scalar(ve[:, :], mv[:, :, 1], EPS, None, ALU.add).then_inc(s_ve, 1)

                def normalise(row, norm, mv, rstd, s_rstd, s_norm):
                    after(dve, s_rstd, row + 1)
                    for t in range(TILES):
                        last = nc.vector.tensor_scalar(norm[:, t * D:(t + 1) * D], x_sb[:, bass.ds(row * S + t * D, D)],
                                                       mv[:, t, 0:1], rstd[:, t:t + 1], ALU.subtract, ALU.mult)
                    last.then_inc(s_norm, 1)

                def step(b, u):
                    if u == 3 and there(b - 1):
                        after(dve, pe_o, b * PAIRS)
                        nc.vector.tensor_scalar(gated[:, :], ps[7][:, :], biasT[:, OB:OB + 1], modT[:, 2, bass.ds(b - 1, 1)],
                                                ALU.add, ALU.mult).then_inc(dve_y, 1)
                    for n, kind, index, row in items(b, u):
                        item(b, n, kind, index, row)
                    row, head = scored(b, u)
                    if there(row):
                        minima(row, head)
                    if u == 4 and there(b - 1):
                        after(dve, pe_yt, b)
                        xr = x_sb[:, bass.ds((b - 1) * S, S)]
                        nc.vector.tensor_tensor(xr, ps[7][:, :], xr, ALU.add).then_inc(dve_x1, 1)
                    row, head = weighted(b, u)
                    if there(row):
                        attended(row, head)
                    if there(b):
                        turned(b, u)
                    row, head = scored(b, u)
                    if there(row):
                        inverse(row, head)
                    if u == 5 and there(b - 1):
                        after(dve, dve_x1, b)
                        moments(b - 1, bn2, mv2, ve2, dve_bn2, dve_ve2)
                    if u == 7 and there(b - 1):
                        normalise(b - 1, norm2, mv2, rstd2, pool_rstd2, dve_norm2)
                    if u == 8 and there(b + 1):
                        moments(b + 1, bn1, mv1, ve1, dve_bn1, dve_ve1)
                    if u == 10 and there(b + 1):
                        normalise(b + 1, norm1, mv1, rstd1, pool_rstd1, dve_norm1)

                dve.wait_ge(ld_x[0], 16)
                for u in range(8, H):
                    step(-1, u)
                dve.wait_ge(ld_x[1], 16)
                for u in range(H):
                    step(0, u)
                with dve.Fori(1, B - 1) as b:
                    for u in range(H):
                        step(b, u)
                for u in range(H):
                    step(B - 1, u)
                for u in range(10):
                    step(B, u)

            @block.gpsimd
            def _(pool):
                nc.gpsimd.memset(ident[:, :], 0.0).then_inc(su_const, 1)
                nc.gpsimd.memset(mask[:, :], 0.0).then_inc(su_const, 1)
                nc.gpsimd.memset(minus_half[:, :], -0.5).then_inc(su_const, 1)
                pool.wait_ge(su_const, 3)
                nc.gpsimd.affine_select(out=ident[:, :], in_=ident[:, :], compare_op=ALU.not_equal, fill=1.0, base=0,
                                        pattern=[[-1, P]], channel_multiplier=1).then_inc(su_const, 1)
                tri = mask[:, S - P:S]
                nc.gpsimd.affine_select(out=tri, in_=tri, compare_op=ALU.is_ge, fill=NEG, base=0,
                                        pattern=[[-1, P]], channel_multiplier=1).then_inc(su_const, 1)
                for part in (pt_hi, pt_lo):
                    for i in range(2):
                        last = nc.gpsimd.memset(part[i][:, PT_OFF[3]:PT_DATA3].bitcast(F32), 0.0)
                    last.then_inc(su_const, 1)

                def step(b, u):
                    if u == 11 and there(b + 1):
                        pool.wait_ge(act_item["h"], b + 2)
                        nc.gpsimd.tensor_tensor(h_lo[:, :], h_f[:, :], h_hi[:, :].bitcast(F32), ALU.subtract).then_inc(pool_hlo, 1)
                    row, head = weighted(b, u)
                    if there(row) and head % 2 == 1:
                        pair = head // 2
                        after(pool, dve_att, row * H + head + 1)
                        after(pool, pe_o, row * PAIRS + pair - 1)
                        pool.sem_inc(pool_waited, 1)
                        nc.gpsimd.tensor_scalar(att_hi[pair % 2][:, :], att[:, :], 1.0, 1.0, ALU.mult, ALU.mult).then_inc(pool_ahi, 1)
                        after(pool, pool_ahi, row * PAIRS + pair + 1)
                        nc.gpsimd.tensor_tensor(att_lo[pair % 2][:, :], att[:, :], att_hi[pair % 2][:, :].bitcast(F32),
                                                ALU.subtract).then_inc(pool_alo, 1)
                    if u == 6 and there(b - 1):
                        after(pool, dve_ve2, b)
                        nc.gpsimd.tensor_tensor(rstd2[:, :], ve2[:, :], minus_half[:, :], ALU.pow).then_inc(pool_rstd2, 1)
                    if u == 9 and there(b + 1):
                        after(pool, dve_ve1, b + 2)
                        nc.gpsimd.tensor_tensor(rstd1[:, :], ve1[:, :], minus_half[:, :], ALU.pow).then_inc(pool_rstd1, 1)
                    row, head = scored(b, u)
                    if there(row):
                        after(pool, dve_rinv, row * H + head + 1)
                        pool.sem_inc(pool_waited, 1)
                        for i in range(TILES):
                            w = slice(P_OFF[i], P_OFF[i + 1])
                            last = nc.gpsimd.tensor_scalar(prob[:, head % 4, w], prob[:, head % 4, w], rinv[:, head % 4, i:i + 1], 1.0,
                                                           ALU.mult, ALU.mult)
                        last.then_inc(pool_prob, 1)

                for u in range(8, H):
                    step(-1, u)
                for u in range(H):
                    step(0, u)
                with pool.Fori(1, B - 1) as b:
                    for u in range(H):
                        step(b, u)
                for u in range(H):
                    step(B - 1, u)
                for u in range(10):
                    step(B, u)

        with ExitStack() as ctx:
            ROWS = 2
            UNITS = ROWS * E
            PAIRED = B // ROWS
            w1_hi = sb(ctx, "w1_hi", [P, E, F], F32R)
            w1_lo = sb(ctx, "w1_lo", [P, E, F], F32R)
            w2_hi = sb(ctx, "w2_hi", [P, E, FC, D], F32R)
            w2_lo = sb(ctx, "w2_lo", [P, E, FC, D], F32R)
            cur = [sb(ctx, f"cur{k}", [P, S]) for k in range(ROWS)]
            cur_hi = [sb(ctx, f"cur_hi{k}", [P, S], F32R) for k in range(ROWS)]
            cur_lo = [sb(ctx, f"cur_lo{k}", [P, S], F32R) for k in range(ROWS)]
            hid = [sb(ctx, f"hid{i}", [P, FC, S]) for i in range(2)]
            hid_hi = [sb(ctx, f"hid_hi{i}", [P, FC, S], F32R) for i in range(2)]
            hid_lo = [sb(ctx, f"hid_lo{i}", [P, FC, S], F32R) for i in range(2)]
            cwb = [sb(ctx, f"cwb{i}", [P, S]) for i in range(2)]
            share = [sb(ctx, f"share{i}", [P, S]) for i in range(2)]
            logit = sb(ctx, "logit", [P, TILES, E])
            gt = sb(ctx, "gt", [P, TILES, E, E])
            eq = sb(ctx, "eq", [P, TILES, E, E])
            rank = sb(ctx, "rank", [P, TILES, E])
            chosen = sb(ctx, "chosen", [P, TILES, E])
            picked = sb(ctx, "picked", [P, TILES, E])
            pair_sum = sb(ctx, "pair_sum", [P, TILES])
            gap = sb(ctx, "gap", [P, TILES, E])
            th = sb(ctx, "th", [P, TILES, E])
            cw2 = sb(ctx, "cw2", [P, TILES, E])
            cw_hl = sb(ctx, "cw_hl", [P, TILES, 2 * E])
            cwT = sb(ctx, "cwT", [2 * E, S], F32R)
            earlier = sb(ctx, "earlier", [P, E, E])
            sel_f = sb(ctx, "sel_f", [2 * E, E, P])
            sel = sb(ctx, "sel", [2 * E, E, P], F32R)
            fin = [sb(ctx, f"fin{k}", [P, S]) for k in range(ROWS)]
            res = [sb(ctx, f"res{k}", [P, S]) for k in range(ROWS)]

            f_const = sem("f_const")
            f_whi = sem("f_whi")
            f_wlo = sem("f_wlo")
            f_sel = sem("f_sel")
            pe_hid = sem("pe_hid")
            pe_y = sem("pe_y")
            pe_gate = sem("pe_gate")
            pe_cwT = sem("pe_cwT")
            pe_cwb = sem("pe_cwb")
            pe_fin = sem("pe_fin")
            act_hid = sem("act_hid")
            act_hi = sem("act_hi")
            act_tanh = sem("act_tanh")
            act_cwT = sem("act_cwT")
            act_cwb = sem("act_cwb")
            act_cur = sem("act_cur")
            dve_hi = sem("dve_hi")
            dve_lo = sem("dve_lo")
            dve_gate = sem("dve_gate")
            dve_share = sem("dve_share")
            dve_fin = sem("dve_fin")
            dve_res = sem("dve_res")
            pool_hi = sem("pool_hi")
            pool_cur = sem("pool_cur")
            pool_chi = sem("pool_chi")
            pool_clo = sem("pool_clo")
            stored = sem("stored")

            FREE_HID = FC
            FREE_LO = 2 * FC
            FREE_Y = 2
            FREE_SHARE = 2
            FREE_CUR = 2
            FREE_FIN = ROWS
            FREE_CWT = 1
            FREE_CWB = 1
            FREE_CLO = 1
            FREE_RES = 1
            GATE = 13
            SPLITS = ROWS * (R + 1)

            def loops(eng, start, body, end):
                with eng.Fori(0, PAIRED) as pb:
                    start(pb)
                    with eng.Fori(0, R) as r:
                        body(pb, r, pb * R + r)
                    end(pb)

            block = ctx.enter_context(nc.Block())

            @block.tensor
            def _(pe):
                def gate(n, pb, r, q):
                    k = n // E
                    pe.wait_ge(pool_clo, pb * SPLITS + r * ROWS + k + 1 + FREE_CLO)
                    pe.wait_ge(act_cwT, q * ROWS + k + FREE_CWT)
                    if n == 0:
                        pe.wait_ge(dve_res, pb * ROWS + FREE_RES)
                    for t in range(TILES):
                        last = nc.tensor.matmul(ps[6][:, t * E:(t + 1) * E], cur[k][:, t * P:(t + 1) * P],
                                                wg_sb[:, bass.ds(r * E, E)], start=True, stop=True)
                    last.then_inc(pe_gate, 1)

                def hidden(n, q):
                    k, e = divmod(n, E)
                    for c in range(FC):
                        pe.wait_ge(act_hid, q * (UNITS * FC) + n * FC + c + 1)
                        w = slice(c * P, (c + 1) * P)
                        nc.tensor.matmul(ps[c][:, :], w1_hi[:, e, w], cur_hi[k][:, :], start=True, stop=False)
                        nc.tensor.matmul(ps[c][:, :], w1_hi[:, e, w], cur_lo[k][:, :], start=False, stop=False)
                        nc.tensor.matmul(ps[c][:, :], w1_lo[:, e, w], cur_hi[k][:, :], start=False, stop=True).then_inc(pe_hid, 1)

                def turn_weights(n, q):
                    k = n // E
                    pe.wait_ge(dve_gate, (q * ROWS + k) * GATE + GATE)
                    for t in range(TILES):
                        last = nc.tensor.transpose(ps[6][0:2 * E, t * P:(t + 1) * P], cw_hl[:, t, :], ident[:, :])
                    last.then_inc(pe_cwT, 1)

                def spread_weights(n, q):
                    k, e = divmod(n, E)
                    pe.wait_ge(act_cwT, q * ROWS + k + 1 + FREE_CWT)
                    pe.wait_ge(act_cwb, q * UNITS + n + FREE_CWB)
                    nc.tensor.matmul(ps[7][:, :], sel[:, e, :], cwT[:, :], start=True, stop=True).then_inc(pe_cwb, 1)

                def expert(n, q):
                    e = n % E
                    pe.wait_ge(dve_share, q * UNITS + n + 1)
                    y = ps[4 + n % 2]
                    for c in range(FC):
                        pe.wait_ge(dve_lo, q * (UNITS * FC) + n * FC + c + 1 + FREE_LO)
                        last = nc.tensor.matmul(y[:, :], w2_hi[:, e, c, :], hid_hi[n % 2][:, c, :], start=(c == 0), stop=False)
                        last = nc.tensor.matmul(y[:, :], w2_hi[:, e, c, :], hid_lo[n % 2][:, c, :], start=False, stop=False)
                        last = nc.tensor.matmul(y[:, :], w2_lo[:, e, c, :], hid_hi[n % 2][:, c, :], start=False, stop=(c == FC - 1))
                    last.then_inc(pe_y, 1)

                def start(pb):
                    pass

                def body(pb, r, q):
                    for n in range(UNITS):
                        if n % E == 0:
                            gate(n, pb, r, q)
                        hidden(n, q)
                        if n % E == 1:
                            turn_weights(n, q)
                        if n:
                            spread_weights(n - 1, q)
                            expert(n - 1, q)
                    spread_weights(UNITS - 1, q)
                    expert(UNITS - 1, q)

                def end(pb):
                    for k in range(ROWS):
                        pe.wait_ge(dve_fin, pb * ROWS + k + 1 + FREE_FIN)
                        if k == 0:
                            pe.wait_ge(act_cwT, (pb + 1) * (R * ROWS) + FREE_CWT)
                        else:
                            pe.wait_ge(act_cwb, (pb + 1) * (R * UNITS) + FREE_CWB)
                        for t in range(TILES):
                            tok = slice(t * P, (t + 1) * P)
                            last = nc.tensor.transpose(ps[6 + k][:, tok], fin[k][:, tok], ident[:, :])
                        last.then_inc(pe_fin, 1)

                pe.sem_inc(pe_y, FREE_Y)
                pe.sem_inc(pe_cwT, FREE_CWT)
                pe.sem_inc(pe_cwb, FREE_CWB)
                pe.wait_ge(f_wlo, 2 * E)
                pe.wait_ge(f_sel, 1)
                loops(pe, start, body, end)

            @block.scalar
            def _(act):
                def gelus(n, q):
                    e = n % E
                    for c in range(FC):
                        g = q * (UNITS * FC) + n * FC + c
                        act.wait_ge(pe_hid, g + 1)
                        act.wait_ge(dve_lo, g + 1)
                        b1 = B1 + e * FC + c
                        nc.scalar.activation(hid[n % 2][:, c, :], ps[c][:, :], ACT.Gelu_apprx_tanh,
                                             bias=biasT[:, b1:b1 + 1]).then_inc(act_hid, 1)

                def highs(n, q):
                    act.wait_ge(pe_y, q * UNITS + n + 1)
                    for c in (0, 1):
                        act.wait_ge(act_hid, q * (UNITS * FC) + n * FC + c + 1 + FREE_HID)
                        nc.scalar.copy(hid_hi[n % 2][:, c, :], hid[n % 2][:, c, :]).then_inc(act_hi, 1)

                def copy_weights(n, q):
                    act.wait_ge(act_tanh, q * ROWS + n // E + 1)
                    act.wait_ge(pe_cwT, q * ROWS + n // E + 1 + FREE_CWT)
                    act.wait_ge(pe_cwb, q * UNITS + (n // E) * E + FREE_CWB)
                    nc.scalar.copy(cwT[:, :], ps[6][0:2 * E, :]).then_inc(act_cwT, 1)

                def copy_spread(n, q):
                    act.wait_ge(pe_cwb, q * UNITS + n + 1 + FREE_CWB)
                    act.wait_ge(dve_share, q * UNITS + n + 1)
                    nc.scalar.copy(cwb[n % 2][:, :], ps[7][:, :]).then_inc(act_cwb, 1)

                def start(pb):
                    act.wait_ge(pool_clo, pb * SPLITS + FREE_CLO)
                    for k in range(ROWS):
                        act.wait_ge(dve_fin, pb * ROWS + k + 1)
                        nc.scalar.copy(cur[k][:, :], cur_all[:, bass.ds((pb * ROWS + k) * S, S)]).then_inc(act_cur, 1)

                def body(pb, r, q):
                    for n in range(UNITS):
                        gelus(n, q)
                        if n % E == 0:
                            act.wait_ge(dve_gate, (q * ROWS + n // E) * GATE + 10)
                            nc.scalar.activation(th[:, :, :], gap[:, :, :], ACT.Tanh).then_inc(act_tanh, 1)
                        highs(n, q)
                        if n % E == 1:
                            copy_weights(n, q)
                        if n:
                            copy_spread(n - 1, q)
                    copy_spread(UNITS - 1, q)

                act.wait_ge(ld_ffn, 16 * (3 + TILES))
                for e in range(E):
                    nc.scalar.copy(w1_hi[:, e, :], w1_raw[:, e * F:(e + 1) * F]).then_inc(f_whi, 1)
                for e in range(E):
                    w = slice(e * FC * D, (e + 1) * FC * D)
                    nc.scalar.copy(w2_hi[:, e, :, :], w2_raw[:, w].rearrange("p (c d) -> p c d", d=D)).then_inc(f_whi, 1)
                act.wait_ge(f_const, 6)
                nc.scalar.copy(sel[:, :, :], sel_f[:, :, :]).then_inc(f_sel, 1)
                act.sem_inc(act_hid, FREE_HID)
                act.sem_inc(act_cwT, FREE_CWT)
                act.sem_inc(act_cwb, FREE_CWB)
                loops(act, start, body, lambda pb: None)

            @block.vector
            def _(dve):
                def gates(n, r, q):
                    base = (q * ROWS + n // E) * GATE
                    by_j = logit[:, :, :].unsqueeze(2).to_broadcast([P, TILES, E, E])
                    by_e = logit[:, :, :].unsqueeze(3).to_broadcast([P, TILES, E, E])
                    dve.wait_ge(pe_gate, q * ROWS + n // E + 1)
                    nc.vector.tensor_tensor(logit[:, :, :], ps[6][:, 0:TILES * E].rearrange("p (t e) -> p t e", e=E),
                                            bg_sb[:, bass.ds(r, 1), :, :].rearrange("p r t e -> p (r t) e"), ALU.add).then_inc(dve_gate, 1)
                    dve.wait_ge(dve_gate, base + 1)
                    nc.vector.tensor_tensor(gt[:, :, :, :], by_j, by_e, ALU.is_gt).then_inc(dve_gate, 1)
                    nc.vector.tensor_tensor(eq[:, :, :, :], by_j, by_e, ALU.is_equal).then_inc(dve_gate, 1)
                    dve.wait_ge(dve_gate, base + 3)
                    nc.vector.tensor_tensor(eq[:, :, :, :], eq[:, :, :, :],
                                            earlier[:, :, :].unsqueeze(1).to_broadcast([P, TILES, E, E]), ALU.mult).then_inc(dve_gate, 1)
                    dve.wait_ge(dve_gate, base + 4)
                    nc.vector.tensor_tensor(gt[:, :, :, :], gt[:, :, :, :], eq[:, :, :, :], ALU.add).then_inc(dve_gate, 1)
                    dve.wait_ge(dve_gate, base + 5)
                    nc.vector.tensor_reduce(rank[:, :, :], gt[:, :, :, :], AX_X, ALU.add).then_inc(dve_gate, 1)
                    dve.wait_ge(dve_gate, base + 6)
                    nc.vector.tensor_scalar(chosen[:, :, :], rank[:, :, :], 2.0, None, ALU.is_lt).then_inc(dve_gate, 1)
                    dve.wait_ge(dve_gate, base + 7)
                    nc.vector.tensor_tensor(picked[:, :, :], logit[:, :, :], chosen[:, :, :], ALU.mult).then_inc(dve_gate, 1)
                    dve.wait_ge(dve_gate, base + 8)
                    nc.vector.tensor_reduce(pair_sum[:, :], picked[:, :, :], AX_X, ALU.add).then_inc(dve_gate, 1)
                    dve.wait_ge(dve_gate, base + 9)
                    nc.vector.scalar_tensor_tensor(out=gap[:, :, :], in0=pair_sum[:, :].unsqueeze(2).to_broadcast([P, TILES, E]),
                                                   scalar=-0.5, in1=logit[:, :, :], op0=ALU.mult, op1=ALU.add).then_inc(dve_gate, 1)

                def weights(n, q):
                    base = (q * ROWS + n // E) * GATE
                    dve.wait_ge(act_tanh, q * ROWS + n // E + 1)
                    nc.vector.scalar_tensor_tensor(out=cw2[:, :, :], in0=th[:, :, :], scalar=1.0, in1=chosen[:, :, :],
                                                   op0=ALU.add, op1=ALU.mult).then_inc(dve_gate, 1)
                    dve.wait_ge(dve_gate, base + 11)
                    dve.wait_ge(pe_cwT, q * ROWS + n // E + FREE_CWT)
                    nc.vector.tensor_scalar(cw_hl[:, :, 0:E].bitcast(F32R), cw2[:, :, :], 0.5, None, ALU.mult).then_inc(dve_gate, 1)
                    dve.wait_ge(dve_gate, base + 12)
                    nc.vector.scalar_tensor_tensor(out=cw_hl[:, :, E:2 * E], in0=cw2[:, :, :], scalar=0.5, in1=cw_hl[:, :, 0:E],
                                                   op0=ALU.mult, op1=ALU.subtract).then_inc(dve_gate, 1)

                def lows(n, q):
                    base = q * (UNITS * FC) + n * FC
                    for c in range(FC):
                        if c < 2:
                            dve.wait_ge(act_hi, q * (UNITS * 2) + n * 2 + c + 1)
                        elif c == 2:
                            dve.wait_ge(pool_hi, q * UNITS + n + 1)
                        else:
                            dve.wait_ge(act_hid, base + c + 1 + FREE_HID)
                            nc.vector.tensor_copy(hid_hi[n % 2][:, c, :], hid[n % 2][:, c, :]).then_inc(dve_hi, 1)
                            dve.wait_ge(dve_hi, q * UNITS + n + 1)
                        nc.vector.tensor_tensor(hid_lo[n % 2][:, c, :], hid[n % 2][:, c, :], hid_hi[n % 2][:, c, :].bitcast(F32),
                                                ALU.subtract).then_inc(dve_lo, 1)

                def shares(n, q):
                    e = n % E
                    dve.wait_ge(pe_y, q * UNITS + n + 1 + FREE_Y)
                    dve.wait_ge(act_cwb, q * UNITS + n + 1 + FREE_CWB)
                    dve.wait_ge(pool_cur, q * UNITS + n + 1)
                    nc.vector.scalar_tensor_tensor(out=share[n % 2][:, :], in0=ps[4 + n % 2][:, :], scalar=biasT[:, B2 + e:B2 + e + 1],
                                                   in1=cwb[n % 2][:, :], op0=ALU.add, op1=ALU.mult).then_inc(dve_share, 1)

                def body(pb, r, q):
                    for n in range(UNITS):
                        if n % E == 0:
                            gates(n, r, q)
                        lows(n, q)
                        if n % E == 0:
                            weights(n, q)
                        if n:
                            shares(n - 1, q)
                    shares(UNITS - 1, q)

                def end(pb):
                    for k in range(ROWS):
                        dve.wait_ge(pool_cur, (pb + 1) * (R * UNITS) - (ROWS - 1 - k) * E + FREE_CUR)
                        nc.vector.tensor_scalar(fin[k][:, :], cur[k][:, :], modT[:, 5, bass.ds(pb * ROWS + k, 1)], None,
                                                ALU.mult).then_inc(dve_fin, 1)
                    dve.wait_ge(stored, pb * (16 * ROWS) + 16 * FREE_RES)
                    for k in range(ROWS):
                        dve.wait_ge(pe_fin, pb * ROWS + k + 1)
                        nc.vector.tensor_tensor(res[k][:, :], ps[6 + k][:, :], x_sb[:, bass.ds((pb * ROWS + k) * S, S)],
                                                ALU.add).then_inc(dve_res, 1)

                for e in range(E):
                    dve.wait_ge(f_whi, e + 1)
                    nc.vector.tensor_tensor(w1_lo[:, e, :], w1_raw[:, e * F:(e + 1) * F], w1_hi[:, e, :].bitcast(F32),
                                            ALU.subtract).then_inc(f_wlo, 1)
                for e in range(E):
                    dve.wait_ge(f_whi, E + e + 1)
                    w = slice(e * FC * D, (e + 1) * FC * D)
                    nc.vector.tensor_tensor(w2_lo[:, e, :, :], w2_raw[:, w].rearrange("p (c d) -> p c d", d=D),
                                            w2_hi[:, e, :, :].bitcast(F32), ALU.subtract).then_inc(f_wlo, 1)
                dve.sem_inc(dve_lo, FREE_LO)
                dve.sem_inc(dve_share, FREE_SHARE)
                dve.sem_inc(dve_fin, FREE_FIN)
                dve.sem_inc(dve_res, FREE_RES)
                dve.wait_ge(f_const, 6)
                loops(dve, lambda pb: None, body, end)

            @block.gpsimd
            def _(pool):
                def split(k, pb, count):
                    pool.sem_inc(pool_waited, 1)
                    nc.gpsimd.tensor_scalar(cur_hi[k][:, :], cur[k][:, :], 1.0, 1.0, ALU.mult, ALU.mult).then_inc(pool_chi, 1)
                    pool.wait_ge(pool_chi, count)
                    nc.gpsimd.tensor_tensor(cur_lo[k][:, :], cur[k][:, :], cur_hi[k][:, :].bitcast(F32), ALU.subtract).then_inc(pool_clo, 1)

                def add(n, pb, r, q):
                    k, e = divmod(n, E)
                    pool.wait_ge(dve_share, q * UNITS + n + 1 + FREE_SHARE)
                    pool.wait_ge(pool_cur, q * UNITS + n + FREE_CUR)
                    nc.gpsimd.tensor_tensor(cur[k][:, :], cur[k][:, :], share[n % 2][:, :], ALU.add).then_inc(pool_cur, 1)
                    if e == E - 1:
                        pool.wait_ge(pool_cur, q * UNITS + n + 1 + FREE_CUR)
                        split(k, pb, pb * SPLITS + (r + 1) * ROWS + k + 1)

                def start(pb):
                    for k in range(ROWS):
                        pool.wait_ge(act_cur, pb * ROWS + k + 1)
                        split(k, pb, pb * SPLITS + k + 1)

                def body(pb, r, q):
                    for n in range(UNITS):
                        pool.wait_ge(pe_y, q * UNITS + n + 1)
                        pool.wait_ge(act_hid, q * (UNITS * FC) + n * FC + 3 + FREE_HID)
                        pool.sem_inc(pool_waited, 1)
                        nc.gpsimd.tensor_scalar(hid_hi[n % 2][:, 2, :], hid[n % 2][:, 2, :], 1.0, 1.0, ALU.mult, ALU.mult).then_inc(pool_hi, 1)
                        if n:
                            add(n - 1, pb, r, q)
                    add(UNITS - 1, pb, r, q)

                nc.gpsimd.memset(earlier[:, :, :], 1.0).then_inc(f_const, 1)
                nc.gpsimd.memset(sel_f[:, :, :], 0.0).then_inc(f_const, 1)
                pool.sem_inc(pool_cur, FREE_CUR)
                pool.sem_inc(pool_clo, FREE_CLO)
                pool.wait_ge(f_const, 2)
                nc.gpsimd.affine_select(out=earlier[:, :, :], in_=earlier[:, :, :], compare_op=ALU.is_gt, fill=0.0, base=0,
                                        pattern=[[1, E], [-1, E]], channel_multiplier=0).then_inc(f_const, 1)
                nc.gpsimd.affine_select(out=sel_f[:, :, :], in_=sel_f[:, :, :], compare_op=ALU.not_equal, fill=1.0, base=0,
                                        pattern=[[-1, E], [0, P]], channel_multiplier=1).then_inc(f_const, 1)
                pool.wait_ge(f_const, 4)
                nc.gpsimd.affine_select(out=sel_f[:, :, :], in_=sel_f[:, :, :], compare_op=ALU.not_equal, fill=1.0, base=-E,
                                        pattern=[[-1, E], [0, P]], channel_multiplier=1).then_inc(f_const, 2)
                loops(pool, start, body, lambda pb: None)

            @block.sync
            def _(sp):
                out_v = out.rearrange("b (t p) d -> b p t d", p=P)
                sp.sem_inc(stored, 16 * FREE_RES)
                with sp.Fori(0, PAIRED) as pb:
                    for k in range(ROWS):
                        sp.wait_ge(dve_res, pb * ROWS + k + 1 + FREE_RES)
                        sp.dma_start(out_v[bass.ds(pb * ROWS + k, 1)].rearrange("b p t d -> p (b t) d"),
                                     res[k][:, :].rearrange("p (t d) -> p t d", d=D)).then_inc(stored, 16)
                sp.wait_ge(stored, 16 * (B + FREE_RES))


_INS = ["L0_attn_x", "L0_attn_Q_w", "L0_attn_Q_b", "L0_attn_K_w", "L0_attn_K_b", "L0_attn_V_w", "L0_attn_V_b", "L0_attn_O_w",
        "L0_attn_O_b", "L0_ffn_Wg", "L0_ffn_bg", "L0_ffn_W1", "L0_ffn_b1", "L0_ffn_W2", "L0_ffn_b2", "L0_c", "L0_wmod"]


def kernel(**inputs):
    import numpy as np
    import concourse.bacc as bacc
    from concourse.bass_utils import run_bass_kernel_spmd

    nc = bacc.Bacc("TRN2", target_bir_lowering=False, num_devices=1)
    arrays, args = {}, []
    for name in _INS:
        a = np.ascontiguousarray(inputs[name])
        arrays["in_" + name] = a
        args.append(nc.dram_tensor("in_" + name, a.shape, mybir.dt.from_np(a.dtype), kind="ExternalInput").ap())
    out = nc.dram_tensor("out_x", inputs["L0_attn_x"].shape, F32, kind="ExternalOutput").ap()
    adaln_block(nc, args, out)
    r = run_bass_kernel_spmd(nc, [arrays], core_ids=[0])
    return r.results[0]["out_x"]
```

```python
from contextlib import ExitStack

import concourse.bass as bass
from concourse import mybir
from concourse.alu_op_type import AluOpType as ALU

ACT = mybir.ActivationFunctionType
F32 = mybir.dt.float32
F32R = mybir.dt.float32r
AX_X = mybir.AxisListType.X

P = 128
EPS = 1e-5
NEG = -1.0e30
BIG = 3.0e38




def adaln_block(nc, ins, out):
    x_d, qw_d, qb_d, kw_d, kb_d, vw_d, vb_d, ow_d, ob_d, wg_d, bg_d, w1_d, b1_d, w2_d, b2_d, c_d, wmod_d = ins
    B, S, D = x_d.shape
    H, _, DH = qw_d.shape
    R, _, E = wg_d.shape
    F = w1_d.shape[2]
    TILES = S // P
    PAIRS = H // 2
    FC = F // P
    SCALE = float(DH) ** -0.5
    assert D == P and DH == 64 and S == 512 and TILES == 4 and H == 16 and E == 4

    P_OFF = [P * (i * (i + 1) // 2) for i in range(TILES + 1)]
    P_COLS = P_OFF[TILES]
    PT_OFF = [0, 512, 1152, 896]
    PT_DATA3 = 1024
    PT_COLS = 1408
    CHUNKS = [
        ([(i, 0) for i in range(4)], 0),
        ([(i, 1) for i in range(1, 4)], 512),
        ([(3, 3), (2, 2), (3, 2)], PT_DATA3),
    ]

    ITEMS = [
        [("q", 2, 0), ("v", 3, 0)],
        [("k", 2, 0)],
        [("q", 3, 0)],
        [("k", 3, 0), ("v", 4, 0)],
        [("q", 4, 0)],
        [("k", 4, 0), ("v", 5, 0)],
        [("q", 5, 0)],
        [("k", 5, 0), ("v", 6, 0)],
        [("q", 6, 0), ("v", 7, 0)],
        [("k", 6, 0), ("h2", 0, -1)],
        [("q", 7, 0)],
        [("k", 7, 0), ("h", 0, 1)],
        [],
        [("q", 0, 1), ("k", 0, 1)],
        [("q", 1, 1), ("v", 0, 1)],
        [("k", 1, 1), ("v", 2, 1), ("v", 1, 1)],
    ]
    ORDER = {
        "pe": [("items", 0), ("scores", 0), ("turn", 0), ("scores", 1), ("turn", 1), ("items", 1),
               ("values", 0), ("scores", 2), ("scores", 3), ("project", 0), ("turn", 2)],
        "act": [("items", 0), ("turn", 0), ("turn", 1), ("scores", 0), ("scores", 1), ("items", 1),
                ("values", 0), ("scores", 2), ("scores", 3), ("turn", 2)],
        "dve": [("scores", 0), ("scores", 1), ("items", 0), ("turn", 0), ("items", 1), ("scores", 2),
                ("scores", 3), ("values", 0), ("turn", 1), ("inverse", 0), ("turn", 2)],
    }
    FLAT = [(step, item) for step in range(H) for item in ITEMS[step]]
    assert len(FLAT) % 2 == 0

    def there(b):
        return not isinstance(b, int) or 0 <= b < B

    with ExitStack() as whole:
        def sb(ctx, name, shape, dt=F32):
            return ctx.enter_context(nc.sbuf_tensor(name, shape, dt))

        def sem(name):
            return whole.enter_context(nc.semaphore(name))

        x_sb = sb(whole, "x_sb", [P, B * TILES * D])
        cur_all = sb(whole, "cur_all", [P, B * S])
        w1_raw = sb(whole, "w1_raw", [P, E * F])
        w2_raw = sb(whole, "w2_raw", [P, E * FC * D])
        ident = sb(whole, "ident", [P, P])
        modT = sb(whole, "modT", [P, 6, B])
        biasT = sb(whole, "biasT", [P, 40])
        wg_sb = sb(whole, "wg_sb", [P, R * E])
        bg_sb = sb(whole, "bg_sb", [P, R, TILES, E])
        NB1 = E * FC
        QB, KB, B1, B2, OB = 0, PAIRS, 2 * PAIRS, 2 * PAIRS + NB1, 2 * PAIRS + NB1 + E
        NROWS = OB + 1

        ps = [whole.enter_context(nc.psum_tensor(f"bank{i}", [P, 512], F32)) for i in range(8)]

        dve_waited = sem("dve_waited")
        pool_waited = sem("pool_waited")

        ld_c = sem("ld_c")
        ld_bias = sem("ld_bias")
        ld_wmod = sem("ld_wmod")
        ld_x = [sem(f"ld_x{i}") for i in range(2)]
        ld_w = sem("ld_w")
        ld_ffn = sem("ld_ffn")

        with ExitStack() as ctx:
            w_names = ["wq", "wk", "wv", "wo"]
            w_hi = {n: sb(ctx, n + "_hi", [P, H * DH], F32R) for n in w_names}
            w_lo = {n: sb(ctx, n + "_lo", [P, H * DH], F32R) for n in w_names}
            v_hl = [sb(ctx, f"v_hl{i}", [P, TILES, H // 2, 2 * DH], F32R) for i in range(2)]
            prob = sb(ctx, "prob", [P, 4, P_COLS])
            neg_s = sb(ctx, "neg_s", [P, P_COLS])
            pt_hi = [sb(ctx, f"pt_hi{i}", [P, PT_COLS], F32R) for i in range(2)]
            pt_lo = [sb(ctx, f"pt_lo{i}", [P, PT_COLS], F32R) for i in range(2)]
            q_hi = [sb(ctx, f"q_hi{i}", [P, S], F32R) for i in range(2)]
            q_lo = [sb(ctx, f"q_lo{i}", [P, S], F32R) for i in range(2)]
            k_hi = [sb(ctx, f"k_hi{i}", [P, S], F32R) for i in range(2)]
            k_lo = [sb(ctx, f"k_lo{i}", [P, S], F32R) for i in range(2)]
            h_f = sb(ctx, "h_f", [P, S])
            h_hi = sb(ctx, "h_hi", [P, S], F32R)
            h_lo = sb(ctx, "h_lo", [P, S], F32R)
            norm1 = sb(ctx, "norm1", [P, TILES * D])
            norm2 = sb(ctx, "norm2", [P, TILES * D])
            gated = sb(ctx, "gated", [P, S])
            att = sb(ctx, "att", [P, S])
            att_hi = [sb(ctx, f"att_hi{i}", [P, S], F32R) for i in range(2)]
            att_lo = [sb(ctx, f"att_lo{i}", [P, S], F32R) for i in range(2)]
            att_small = sb(ctx, "att_small", [DH, S])
            mask = sb(ctx, "mask", [P, S])
            negmax = sb(ctx, "negmax", [P, TILES])
            sums = sb(ctx, "sums", [P, 4, TILES])
            rinv = sb(ctx, "rinv", [P, 4, TILES])
            bn1 = sb(ctx, "bn1", [P, TILES, 6])
            bn2 = sb(ctx, "bn2", [P, TILES, 6])
            mv1 = sb(ctx, "mv1", [P, TILES, 2])
            mv2 = sb(ctx, "mv2", [P, TILES, 2])
            ve1 = sb(ctx, "ve1", [P, TILES])
            ve2 = sb(ctx, "ve2", [P, TILES])
            rstd1 = sb(ctx, "rstd1", [P, TILES])
            rstd2 = sb(ctx, "rstd2", [P, TILES])
            minus_half = sb(ctx, "minus_half", [P, TILES])
            vbT = sb(ctx, "vbT", [DH, H])
            raw = {n: prob[:, i, 0:H * DH] for i, n in enumerate(w_names)}
            wmod_raw = cur_all[:, 0:6 * D]
            c_sb = cur_all[0:B, 1024:1024 + D]
            c_act = cur_all[0:B, 1152:1152 + D]
            c_tanh = cur_all[0:B, 1280:1280 + D]
            siluT = cur_all[:, 1408:1408 + B]
            rows = cur_all[0:NROWS, 1536:1536 + P]
            vb_rows = cur_all[0:H, 1664:1664 + DH]
            ga_pos = cur_all[:, 1792:1792 + 2 * B]
            ga_neg = cur_all[:, 1856:1856 + 2 * B]

            su_const = sem("su_const")
            su_tanh = sem("su_tanh")
            su_dve = sem("su_dve")
            su_pe = sem("su_pe")
            su_whi = sem("su_whi")
            su_wlo = sem("su_wlo")
            pe_item = {n: sem("pe_" + n) for n in ("q", "k", "v", "h", "h2")}
            pe_s = sem("pe_s")
            pe_t = sem("pe_t")
            pe_pv = sem("pe_pv")
            pe_o = sem("pe_o")
            pe_yt = sem("pe_yt")
            act_item = {n: sem("act_" + n) for n in ("q", "k", "v", "h")}
            act_exp = sem("act_exp")
            act_pt = sem("act_pt")
            act_small = sem("act_small")
            dve_item = {n: sem("dve_" + n) for n in ("q", "k", "v", "h", "h2")}
            dve_min = sem("dve_min")
            dve_pt = sem("dve_pt")
            dve_rinv = sem("dve_rinv")
            dve_att = sem("dve_att")
            dve_y = sem("dve_y")
            dve_x1 = sem("dve_x1")
            dve_bn1 = sem("dve_bn1")
            dve_bn2 = sem("dve_bn2")
            dve_ve1 = sem("dve_ve1")
            dve_ve2 = sem("dve_ve2")
            dve_norm1 = sem("dve_norm1")
            dve_norm2 = sem("dve_norm2")
            pool_hlo = sem("pool_hlo")
            pool_prob = sem("pool_prob")
            pool_ahi = sem("pool_ahi")
            pool_alo = sem("pool_alo")
            pool_rstd1 = sem("pool_rstd1")
            pool_rstd2 = sem("pool_rstd2")

            def after(eng, s, n):
                if not isinstance(n, int) or n > 0:
                    eng.wait_ge(s, n)

            def nth(kind, index, b):
                per_row = {"q": PAIRS, "k": PAIRS, "v": 2 * TILES, "h": 1, "h2": 1}[kind]
                return b * per_row + index + 1

            def bank_of(n):
                return ps[n % 2]

            def bank_free(eng, n, b):
                back = n - 2
                while True:
                    step, (kind, index, rel) = FLAT[back % len(FLAT)]
                    row = b + rel + (back // len(FLAT))
                    if there(row):
                        break
                    back -= 2
                    if back < -2 * len(FLAT):
                        return
                after(eng, dve_item[kind], nth(kind, index, row))

            first = {}
            for n, (step, item) in enumerate(FLAT):
                first.setdefault(step, n)

            def items(b, u):
                return [(first[u] + i, kind, index, b + rel)
                        for i, (kind, index, rel) in enumerate(ITEMS[u]) if there(b + rel)]

            def scored(b, u):
                return (b, u + 2) if u + 2 < H else (b + 1, u + 2 - H)

            def weighted(b, u):
                return (b, u - 1) if u else (b - 1, H - 1)

            block = ctx.enter_context(nc.Block())

            @block.sync
            def _(sp):
                sp.dma_start(c_sb, c_d).then_inc(ld_c, 16)
                xv = x_d.rearrange("b (t p) d -> p (b t) d", p=P)
                xs = x_sb[:, :].rearrange("p (n d) -> p n d", d=D)
                sp.dma_start(xs[:, 0:TILES, :], xv[:, 0:TILES, :]).then_inc(ld_x[0], 16)
                sp.dma_start(wmod_raw, wmod_d).then_inc(ld_wmod, 16)
                for n, d in (("wq", qw_d), ("wk", kw_d), ("wv", vw_d)):
                    sp.dma_start(raw[n].rearrange("p (h d) -> p h d", d=DH), d.rearrange("h m d -> m h d")).then_inc(ld_w, 16)
                sp.dma_start(raw["wo"].rearrange("p (n m) -> p n m", m=D),
                             ow_d.rearrange("(n two) d m -> (two d) n m", two=2)).then_inc(ld_w, 16)
                sp.dma_start(xs[:, TILES:, :], xv[:, TILES:, :]).then_inc(ld_x[1], 16)
                sp.dma_start(w1_raw[:, :].rearrange("p (e f) -> p e f", e=E), w1_d.rearrange("e h f -> h e f")).then_inc(ld_ffn, 16)
                sp.dma_start(w2_raw[:, :].rearrange("p (e c h) -> p e c h", e=E, c=FC),
                             w2_d.rearrange("e (c p) h -> p e c h", p=P)).then_inc(ld_ffn, 16)
                sp.dma_start(wg_sb[:, :].rearrange("p (r e) -> p r e", r=R), wg_d.rearrange("r h e -> h r e")).then_inc(ld_ffn, 16)
                for t in range(TILES):
                    sp.dma_start(bg_sb[:, :, t, :], bg_d.partition_broadcast(P)).then_inc(ld_ffn, 16)

            @block.tensor
            def _(pe):
                def three(out_ap, lhs_hi, lhs_lo, rhs_hi, rhs_lo, start=True, stop=True):
                    nc.tensor.matmul(out_ap, lhs_hi, rhs_hi, start=start, stop=False)
                    nc.tensor.matmul(out_ap, lhs_hi, rhs_lo, start=False, stop=False)
                    return nc.tensor.matmul(out_ap, lhs_lo, rhs_hi, start=False, stop=stop)

                pe.wait_ge(su_const, 4)
                pe.wait_ge(ld_bias, 16 * 6)
                nc.tensor.transpose(ps[2][:, 0:NROWS], rows, ident[0:NROWS, 0:NROWS])
                nc.tensor.transpose(ps[2][0:DH, 64:64 + H], vb_rows, ident[0:H, 0:H])
                pe.wait_ge(su_dve, 1)
                nc.tensor.transpose(ps[2][:, 128:128 + B], c_act, ident[0:B, 0:B]).then_inc(su_pe, 1)
                pe.wait_ge(su_dve, 2)
                pe.wait_ge(ld_wmod, 16)
                for j in range(6):
                    last = nc.tensor.matmul(ps[3][:, j * B:(j + 1) * B], wmod_raw[:, j * D:(j + 1) * D], siluT, start=True, stop=True)
                last.then_inc(su_pe, 1)

                def item(b, n, kind, index, row):
                    bank_free(pe, n, b)
                    bank = bank_of(n)
                    done = pe_item[kind]
                    if kind in ("q", "k"):
                        if kind == "q" and index == 0:
                            pe.wait_ge(pool_hlo, row + 1)
                            pe.wait_ge(su_wlo, 4)
                        w = slice(index * P, (index + 1) * P)
                        name = "w" + kind
                        three(bank[:, :], w_hi[name][:, w], w_lo[name][:, w], h_hi[:, :], h_lo[:, :]).then_inc(done, 1)
                    if kind == "v":
                        half, t = divmod(index, TILES)
                        tok, cols = slice(t * P, (t + 1) * P), slice(half * 512, (half + 1) * 512)
                        three(bank[:, :], h_hi[:, tok], h_lo[:, tok], w_hi["wv"][:, cols], w_lo["wv"][:, cols]).then_inc(done, 1)
                    if kind in ("h", "h2"):
                        src = norm1 if kind == "h" else norm2
                        pe.wait_ge(dve_norm1 if kind == "h" else dve_norm2, row + 1)
                        for t in range(TILES):
                            tok = slice(t * P, (t + 1) * P)
                            last = nc.tensor.transpose(bank[:, tok], src[:, tok], ident[:, :])
                        last.then_inc(done, 1)

                def scores(b, u, i):
                    pair, lo = u // 2, DH * (u % 2)
                    half = slice(lo, lo + DH)
                    if u % 2 == 0 and i == 0:
                        after(pe, dve_item["q"], nth("q", pair, b))
                        after(pe, dve_item["k"], nth("k", pair, b))
                    after(pe, dve_min, (b * H + u) * TILES + i - 1)
                    tok, keys = slice(i * P, (i + 1) * P), slice(0, max(256, (i + 1) * P))
                    three(ps[2 + i % 2][:, keys], q_hi[pair % 2][half, tok], q_lo[pair % 2][half, tok],
                          k_hi[pair % 2][half, keys], k_lo[pair % 2][half, keys]).then_inc(pe_s, 1)

                def values(b, u):
                    pair = u // 2
                    if u % (H // 2) == 0:
                        after(pe, dve_item["v"], nth("v", TILES * (u * 2 // H) + TILES - 1, b))
                    after(pe, dve_pt, (b * H + u) * 3 + 3)
                    after(pe, dve_att, b * H + u)
                    for j in (0, 1, 2, 3):
                        width = max(256, S - j * P)
                        stat = v_hl[u * 2 // H][:, j, u % (H // 2), :]
                        cols = slice(PT_OFF[j], PT_OFF[j] + width)
                        for n, part in enumerate((pt_hi, pt_lo)):
                            last = nc.tensor.matmul(ps[6][:, S - width:S], stat, part[u % 2][:, cols],
                                                    start=(j == 0 and n == 0), stop=(j == 3 and n == 1))
                    last.then_inc(pe_pv, 1)

                def turn(b, u, c):
                    if c == 0:
                        after(pe, pool_prob, b * H + u + 1)
                    after(pe, dve_pt, (b * H + u) * 3 + c - 1)
                    bank = ps[4 + (u * 3 + c) % 2]
                    for z, (i, j) in enumerate(CHUNKS[c][0]):
                        col = P_OFF[i] + j * P
                        last = nc.tensor.transpose(bank[:, z * P:(z + 1) * P], prob[:, u % 4, col:col + P], ident[:, :])
                    last.then_inc(pe_t, 1)

                def project(b, pair):
                    after(pe, pool_alo, b * PAIRS + pair + 1)
                    if pair == 0:
                        after(pe, dve_x1, b)
                    w = slice(pair * D, (pair + 1) * D)
                    three(ps[7][:, :], w_hi["wo"][:, w], w_lo["wo"][:, w], att_hi[pair % 2][:, :], att_lo[pair % 2][:, :],
                          start=(pair == 0), stop=(pair == PAIRS - 1)).then_inc(pe_o, 1)

                def step(b, u):
                    if u == 4 and there(b - 1):
                        after(pe, dve_y, b)
                        for t in range(TILES):
                            tok = slice(t * P, (t + 1) * P)
                            last = nc.tensor.transpose(ps[7][:, tok], gated[:, tok], ident[:, :])
                        last.then_inc(pe_yt, 1)
                    todo = items(b, u)
                    for part, i in ORDER["pe"]:
                        if part == "scores" and there(scored(b, u)[0]):
                            scores(*scored(b, u), i)
                        if part == "turn" and there(b):
                            turn(b, u, i)
                        if part == "values" and there(weighted(b, u)[0]):
                            values(*weighted(b, u))
                        if part == "items":
                            for what in (todo[1:] if i else todo[:1]):
                                item(b, *what)
                        if part == "project":
                            if u == 0 and there(b - 1):
                                project(b - 1, PAIRS - 2)
                            if u == 2 and there(b - 1):
                                project(b - 1, PAIRS - 1)
                            if u >= 4 and u % 2 == 0 and there(b):
                                project(b, (u - 4) // 2)

                for u in range(8, H):
                    step(-1, u)
                for u in range(H):
                    step(0, u)
                with pe.Fori(1, B - 1) as b:
                    for u in range(H):
                        step(b, u)
                for u in range(H):
                    step(B - 1, u)
                for u in range(10):
                    step(B, u)

            @block.scalar
            def _(act):
                act.dma_start(rows[QB:QB + PAIRS, :], qb_d.rearrange("(n two) d -> n (two d)", two=2)).then_inc(ld_bias, 16)
                act.dma_start(rows[KB:KB + PAIRS, :], kb_d.rearrange("(n two) d -> n (two d)", two=2)).then_inc(ld_bias, 16)
                act.dma_start(rows[B1:B1 + NB1, :], b1_d.rearrange("e (c f) -> (e c) f", f=P)).then_inc(ld_bias, 16)
                act.dma_start(rows[B2:B2 + E, :], b2_d).then_inc(ld_bias, 16)
                act.dma_start(rows[OB:OB + 1, :], ob_d.rearrange("(a m) -> a m", a=1)).then_inc(ld_bias, 16)
                act.dma_start(vb_rows, vb_d).then_inc(ld_bias, 16)
                act.wait_ge(ld_c, 16)
                nc.scalar.activation(c_tanh, c_sb, ACT.Tanh, scale=0.5).then_inc(su_tanh, 1)
                for n, name in enumerate(w_names):
                    act.wait_ge(ld_w, 16 * 4)
                    nc.scalar.copy(w_hi[name][:, :], raw[name]).then_inc(su_whi, 1)

                def item(b, n, kind, index, row):
                    bank = bank_of(n)
                    if kind in ("q", "k"):
                        act.wait_ge(pe_item[kind], nth(kind, index, row))
                        hi, col = (q_hi, QB) if kind == "q" else (k_hi, KB)
                        nc.scalar.activation(hi[index % 2][:, :], bank[:, :], ACT.Identity,
                                             bias=biasT[:, col + index:col + index + 1]).then_inc(act_item[kind], 1)
                    if kind == "v":
                        half, t = divmod(index, TILES)
                        act.wait_ge(pe_item["v"], nth("v", index, row))
                        nc.scalar.copy(v_hl[half][:, t, :, 0:DH],
                                       bank[:, :].rearrange("p (h d) -> p h d", d=DH)).then_inc(act_item["v"], 1)
                    if kind == "h":
                        act.wait_ge(dve_item["h"], row + 1)
                        nc.scalar.copy(h_hi[:, :], h_f[:, :]).then_inc(act_item["h"], 1)

                def exps(b, u, i):
                    after(act, dve_min, (b * H + u) * TILES + i + 1)
                    w = slice(P_OFF[i], P_OFF[i + 1])
                    nc.scalar.activation(prob[:, u % 4, w], neg_s[:, w], ACT.Exp, scale=-1.0,
                                         bias=negmax[:, i:i + 1], accum_out=sums[:, u % 4, i:i + 1]).then_inc(act_exp, 1)

                def small(b, u):
                    after(act, pe_pv, b * H + u + 1)
                    nc.scalar.copy(att_small[:, :], ps[6][DH:P, :]).then_inc(act_small, 1)

                def turned(b, u, c):
                    after(act, pe_t, (b * H + u) * 3 + c + 1)
                    dst, width = CHUNKS[c][1], len(CHUNKS[c][0]) * P
                    nc.scalar.copy(pt_hi[u % 2][:, dst:dst + width],
                                   ps[4 + (u * 3 + c) % 2][:, 0:width]).then_inc(act_pt, 1)

                def step(b, u):
                    todo = items(b, u)
                    for part, i in ORDER["act"]:
                        if part == "scores" and there(scored(b, u)[0]):
                            exps(*scored(b, u), i)
                        if part == "turn" and there(b):
                            turned(b, u, i)
                        if part == "values" and there(weighted(b, u)[0]):
                            small(*weighted(b, u))
                        if part == "items":
                            for what in (todo[1:] if i else todo[:1]):
                                item(b, *what)

                act.wait_ge(su_wlo, 4)
                act.wait_ge(su_dve, 6)
                for u in range(8, H):
                    step(-1, u)
                for u in range(H):
                    step(0, u)
                with act.Fori(1, B - 1) as b:
                    for u in range(H):
                        step(b, u)
                for u in range(H):
                    step(B - 1, u)
                for u in range(10):
                    step(B, u)

            @block.vector
            def _(dve):
                dve.wait_ge(su_tanh, 1)
                nc.vector.scalar_tensor_tensor(out=c_act, in0=c_tanh, scalar=1.0, in1=c_sb, op0=ALU.add, op1=ALU.mult).then_inc(su_dve, 1)
                dve.wait_ge(su_pe, 1)
                nc.vector.tensor_scalar(siluT, ps[2][:, 128:128 + B], 0.5, None, ALU.mult).then_inc(su_dve, 1)
                nc.vector.tensor_copy(biasT[:, 0:NROWS], ps[2][:, 0:NROWS])
                nc.vector.tensor_copy(vbT[:, :], ps[2][0:DH, 64:64 + H])
                dve.wait_ge(su_pe, 2)
                nc.vector.tensor_copy(modT[:, :, :], ps[3][:, 0:6 * B].rearrange("p (j b) -> p j b", b=B)).then_inc(su_dve, 1)
                dve.wait_ge(su_dve, 3)
                g = modT[:, 2:6:3, :]
                ga_pos_v = ga_pos.rearrange("p (j b) -> p j b", b=B)
                ga_neg_v = ga_neg.rearrange("p (j b) -> p j b", b=B)
                nc.vector.tensor_scalar(ga_pos_v, g, 0.0, 2.0, ALU.is_ge, ALU.mult)
                nc.vector.tensor_scalar(ga_neg_v, g, -1.0, None, ALU.mult)
                nc.vector.tensor_scalar(modT[:, 1:5:3, :], modT[:, 1:5:3, :], 1.0, None, ALU.add).then_inc(su_dve, 1)
                dve.wait_ge(su_dve, 4)
                nc.vector.tensor_scalar(ga_pos_v, ga_pos_v, 1.0, None, ALU.subtract)
                nc.vector.tensor_tensor(ga_neg_v, ga_neg_v, g, ALU.max).then_inc(su_dve, 1)
                dve.wait_ge(su_dve, 5)
                nc.vector.scalar_tensor_tensor(out=g, in0=ga_neg_v, scalar=0.25, in1=ga_pos_v, op0=ALU.max, op1=ALU.mult).then_inc(su_dve, 1)
                for n, name in enumerate(w_names):
                    dve.wait_ge(su_whi, n + 1)
                    nc.vector.tensor_tensor(w_lo[name][:, :], raw[name], w_hi[name][:, :].bitcast(F32), ALU.subtract).then_inc(su_wlo, 1)
                dve.wait_ge(su_dve, 6)
                dve.wait_ge(su_const, 7)

                def item(b, n, kind, index, row):
                    bank = bank_of(n)
                    if kind in ("q", "k"):
                        hi, lo, col = (q_hi, q_lo, QB) if kind == "q" else (k_hi, k_lo, KB)
                        dve.wait_ge(act_item[kind], nth(kind, index, row))
                        nc.vector.scalar_tensor_tensor(out=lo[index % 2][:, :], in0=bank[:, :], scalar=biasT[:, col + index:col + index + 1],
                                                       in1=hi[index % 2][:, :].bitcast(F32), op0=ALU.add, op1=ALU.subtract).then_inc(dve_item[kind], 1)
                    if kind == "v":
                        half, t = divmod(index, TILES)
                        dve.wait_ge(act_item["v"], nth("v", index, row))
                        nc.vector.tensor_tensor(v_hl[half][:, t, :, DH:2 * DH], bank[:, :].rearrange("p (h d) -> p h d", d=DH),
                                                v_hl[half][:, t, :, 0:DH].bitcast(F32), ALU.subtract).then_inc(dve_item["v"], 1)
                    if kind == "h":
                        dve.wait_ge(pe_item["h"], row + 1)
                        after(dve, pool_hlo, row)
                        nc.vector.tensor_scalar(h_f[:, :], bank[:, :], modT[:, 1, bass.ds(row, 1)], modT[:, 0, bass.ds(row, 1)],
                                                ALU.mult, ALU.add).then_inc(dve_item["h"], 1)
                    if kind == "h2":
                        dve.wait_ge(pe_item["h2"], row + 1)
                        nc.vector.tensor_scalar(cur_all[:, bass.ds(row * S, S)], bank[:, :], modT[:, 4, bass.ds(row, 1)],
                                                modT[:, 3, bass.ds(row, 1)], ALU.mult, ALU.add).then_inc(dve_item["h2"], 1)

                def minima(b, u, i):
                    after(dve, pe_s, (b * H + u) * TILES + i + 1)
                    dve.sem_inc(dve_waited, 1)
                    w = (i + 1) * P
                    nc.vector.tensor_tensor_reduce(neg_s[:, P_OFF[i]:P_OFF[i + 1]], ps[2 + i % 2][:, 0:w], mask[:, S - w:S],
                                                   -SCALE, BIG, ALU.add, ALU.min, negmax[:, i:i + 1]).then_inc(dve_min, 1)

                def attended(b, u):
                    after(dve, act_small, b * H + u + 1)
                    if u % 2 == 0:
                        after(dve, pool_alo, b * PAIRS + u // 2)
                    r = DH * (u % 2)
                    nc.vector.scalar_tensor_tensor(out=att[r:r + DH, :], in0=ps[6][0:DH, :], scalar=vbT[:, u:u + 1], in1=att_small[:, :],
                                                   op0=ALU.add, op1=ALU.add).then_inc(dve_att, 1)

                def turned(b, u, c):
                    after(dve, act_pt, (b * H + u) * 3 + c + 1)
                    dst, width = CHUNKS[c][1], len(CHUNKS[c][0]) * P
                    nc.vector.tensor_tensor(pt_lo[u % 2][:, dst:dst + width], ps[4 + (u * 3 + c) % 2][:, 0:width],
                                            pt_hi[u % 2][:, dst:dst + width].bitcast(F32), ALU.subtract).then_inc(dve_pt, 1)

                def inverse(b, u):
                    after(dve, act_exp, (b * H + u + 1) * TILES)
                    nc.vector.reciprocal(rinv[:, u % 4, :], sums[:, u % 4, :]).then_inc(dve_rinv, 1)

                def moments(row, stats, mv, ve, s_bn, s_ve):
                    dve.sem_inc(dve_waited, 1)
                    for t in range(TILES):
                        last = nc.vector.bn_stats(stats[:, t, :], x_sb[:, bass.ds(row * S + t * D, D)])
                    last.then_inc(s_bn, 1)
                    after(dve, s_bn, row * 2 + 1)
                    dve.sem_inc(dve_waited, 1)
                    for t in range(TILES):
                        last = nc.vector.bn_aggr(mv[:, t, :], stats[:, t, :])
                    last.then_inc(s_bn, 1)
                    after(dve, s_bn, row * 2 + 2)
                    nc.vector.tensor_scalar(ve[:, :], mv[:, :, 1], EPS, None, ALU.add).then_inc(s_ve, 1)

                def normalise(row, norm, mv, rstd, s_rstd, s_norm):
                    after(dve, s_rstd, row + 1)
                    for t in range(TILES):
                        last = nc.vector.tensor_scalar(norm[:, t * D:(t + 1) * D], x_sb[:, bass.ds(row * S + t * D, D)],
                                                       mv[:, t, 0:1], rstd[:, t:t + 1], ALU.subtract, ALU.mult)
                    last.then_inc(s_norm, 1)

                def step(b, u):
                    if u == 3 and there(b - 1):
                        after(dve, pe_o, b * PAIRS)
                        nc.vector.tensor_scalar(gated[:, :], ps[7][:, :], biasT[:, OB:OB + 1], modT[:, 2, bass.ds(b - 1, 1)],
                                                ALU.add, ALU.mult).then_inc(dve_y, 1)
                    todo = items(b, u)
                    if u == 4 and there(b - 1):
                        after(dve, pe_yt, b)
                        xr = x_sb[:, bass.ds((b - 1) * S, S)]
                        nc.vector.tensor_tensor(xr, ps[7][:, :], xr, ALU.add).then_inc(dve_x1, 1)
                    for part, i in ORDER["dve"]:
                        if part == "scores" and there(scored(b, u)[0]):
                            minima(*scored(b, u), i)
                        if part == "turn" and there(b):
                            turned(b, u, i)
                        if part == "values" and there(weighted(b, u)[0]):
                            attended(*weighted(b, u))
                        if part == "items":
                            for what in (todo[1:] if i else todo[:1]):
                                item(b, *what)
                        if part == "inverse" and there(scored(b, u)[0]):
                            inverse(*scored(b, u))
                    if u == 5 and there(b - 1):
                        after(dve, dve_x1, b)
                        moments(b - 1, bn2, mv2, ve2, dve_bn2, dve_ve2)
                    if u == 7 and there(b - 1):
                        normalise(b - 1, norm2, mv2, rstd2, pool_rstd2, dve_norm2)
                    if u == 8 and there(b + 1):
                        moments(b + 1, bn1, mv1, ve1, dve_bn1, dve_ve1)
                    if u == 10 and there(b + 1):
                        normalise(b + 1, norm1, mv1, rstd1, pool_rstd1, dve_norm1)

                dve.wait_ge(ld_x[0], 16)
                for u in range(8, H):
                    step(-1, u)
                dve.wait_ge(ld_x[1], 16)
                for u in range(H):
                    step(0, u)
                with dve.Fori(1, B - 1) as b:
                    for u in range(H):
                        step(b, u)
                for u in range(H):
                    step(B - 1, u)
                for u in range(10):
                    step(B, u)

            @block.gpsimd
            def _(pool):
                nc.gpsimd.memset(ident[:, :], 0.0).then_inc(su_const, 1)
                nc.gpsimd.memset(mask[:, :], 0.0).then_inc(su_const, 1)
                nc.gpsimd.memset(minus_half[:, :], -0.5).then_inc(su_const, 1)
                pool.wait_ge(su_const, 3)
                nc.gpsimd.affine_select(out=ident[:, :], in_=ident[:, :], compare_op=ALU.not_equal, fill=1.0, base=0,
                                        pattern=[[-1, P]], channel_multiplier=1).then_inc(su_const, 1)
                tri = mask[:, S - P:S]
                nc.gpsimd.affine_select(out=tri, in_=tri, compare_op=ALU.is_ge, fill=NEG, base=0,
                                        pattern=[[-1, P]], channel_multiplier=1).then_inc(su_const, 1)
                for part in (pt_hi, pt_lo):
                    for i in range(2):
                        last = nc.gpsimd.memset(part[i][:, PT_OFF[3]:PT_DATA3].bitcast(F32), 0.0)
                    last.then_inc(su_const, 1)

                def step(b, u):
                    if u == 11 and there(b + 1):
                        pool.wait_ge(act_item["h"], b + 2)
                        nc.gpsimd.tensor_tensor(h_lo[:, :], h_f[:, :], h_hi[:, :].bitcast(F32), ALU.subtract).then_inc(pool_hlo, 1)
                    row, head = weighted(b, u)
                    if there(row) and head % 2 == 1:
                        pair = head // 2
                        after(pool, dve_att, row * H + head + 1)
                        pool.sem_inc(pool_waited, 1)
                        nc.gpsimd.tensor_scalar(att_hi[pair % 2][:, :], att[:, :], 1.0, 1.0, ALU.mult, ALU.mult).then_inc(pool_ahi, 1)
                        after(pool, pool_ahi, row * PAIRS + pair + 1)
                        nc.gpsimd.tensor_tensor(att_lo[pair % 2][:, :], att[:, :], att_hi[pair % 2][:, :].bitcast(F32),
                                                ALU.subtract).then_inc(pool_alo, 1)
                    if u == 6 and there(b - 1):
                        after(pool, dve_ve2, b)
                        nc.gpsimd.tensor_tensor(rstd2[:, :], ve2[:, :], minus_half[:, :], ALU.pow).then_inc(pool_rstd2, 1)
                    if u == 9 and there(b + 1):
                        after(pool, dve_ve1, b + 2)
                        nc.gpsimd.tensor_tensor(rstd1[:, :], ve1[:, :], minus_half[:, :], ALU.pow).then_inc(pool_rstd1, 1)
                    row, head = scored(b, u)
                    if there(row):
                        after(pool, dve_rinv, row * H + head + 1)
                        pool.sem_inc(pool_waited, 1)
                        for i in range(TILES):
                            w = slice(P_OFF[i], P_OFF[i + 1])
                            last = nc.gpsimd.tensor_scalar(prob[:, head % 4, w], prob[:, head % 4, w], rinv[:, head % 4, i:i + 1], 1.0,
                                                           ALU.mult, ALU.mult)
                        last.then_inc(pool_prob, 1)

                for u in range(8, H):
                    step(-1, u)
                for u in range(H):
                    step(0, u)
                with pool.Fori(1, B - 1) as b:
                    for u in range(H):
                        step(b, u)
                for u in range(H):
                    step(B - 1, u)
                for u in range(10):
                    step(B, u)

        with ExitStack() as ctx:
            ROWS = 2
            UNITS = ROWS * E
            PAIRED = B // ROWS
            ACT_SPLITS, POOL_SPLITS = (0, 1), (2, 3)
            assert E == 4 and PAIRED * ROWS == B and R > 2
            w1_hi = sb(ctx, "w1_hi", [P, E, F], F32R)
            w1_lo = sb(ctx, "w1_lo", [P, E, F], F32R)
            w2_hi = sb(ctx, "w2_hi", [P, E, FC, D], F32R)
            w2_lo = sb(ctx, "w2_lo", [P, E, FC, D], F32R)
            cur = [sb(ctx, f"cur{k}", [P, S]) for k in range(ROWS)]
            cur_hi = [sb(ctx, f"cur_hi{k}", [P, S], F32R) for k in range(ROWS)]
            cur_lo = [sb(ctx, f"cur_lo{k}", [P, S], F32R) for k in range(ROWS)]
            hid = [sb(ctx, f"hid{i}", [P, FC, S]) for i in range(2)]
            hid_hi = [sb(ctx, f"hid_hi{i}", [P, FC, S], F32R) for i in range(2)]
            hid_lo = [sb(ctx, f"hid_lo{i}", [P, FC, S], F32R) for i in range(2)]
            cwb = [sb(ctx, f"cwb{i}", [P, S]) for i in range(2)]
            share = [sb(ctx, f"share{i}", [P, S]) for i in range(2)]
            logit = sb(ctx, "logit", [P, TILES, E])
            gt = sb(ctx, "gt", [P, TILES, E, E])
            eq = sb(ctx, "eq", [P, TILES, E, E])
            rank = sb(ctx, "rank", [P, TILES, E])
            chosen = sb(ctx, "chosen", [P, TILES, E])
            picked = sb(ctx, "picked", [P, TILES, E])
            pair_sum = sb(ctx, "pair_sum", [P, TILES])
            gap = sb(ctx, "gap", [P, TILES, E])
            th = sb(ctx, "th", [P, TILES, E])
            cw2 = sb(ctx, "cw2", [P, TILES, E])
            cw_hl = sb(ctx, "cw_hl", [P, TILES, 2 * E])
            cwT = sb(ctx, "cwT", [2 * E, S], F32R)
            earlier = sb(ctx, "earlier", [P, E, E])
            sel_f = sb(ctx, "sel_f", [2 * E, E, P])
            sel = sb(ctx, "sel", [2 * E, E, P], F32R)
            fin = [sb(ctx, f"fin{k}", [P, S]) for k in range(ROWS)]

            f_const = sem("f_const")
            f_sel = sem("f_sel")
            act_whi = sem("act_whi")
            dve_wlo = sem("dve_wlo")
            pool_whi = sem("pool_whi")
            pool_wlo = sem("pool_wlo")
            pe_hid = sem("pe_hid")
            pe_y = sem("pe_y")
            pe_gate = sem("pe_gate")
            pe_cwT = sem("pe_cwT")
            pe_cwb = sem("pe_cwb")
            pe_fin = sem("pe_fin")
            act_hid = sem("act_hid")
            act_hi = sem("act_hi")
            act_tanh = sem("act_tanh")
            act_cwT = sem("act_cwT")
            act_cwb = sem("act_cwb")
            act_cur = sem("act_cur")
            dve_hi = sem("dve_hi")
            dve_lo = sem("dve_lo")
            dve_gate = sem("dve_gate")
            dve_share = sem("dve_share")
            dve_fin = sem("dve_fin")
            dve_res = sem("dve_res")
            pool_cur = sem("pool_cur")
            pool_chi = sem("pool_chi")
            pool_clo = sem("pool_clo")
            stored = sem("stored")

            GATE = 13

            def after(eng, s, n):
                if not isinstance(n, int) or n > 0:
                    eng.wait_ge(s, n)

            def loops(eng, body):
                body(0, 0, 0, True, False)
                with eng.Fori(0, PAIRED - 1) as pb:
                    with eng.Fori(1, R - 1) as r:
                        body(pb, r, pb * R + r, False, False)
                    body(pb, R - 1, pb * R + R - 1, False, True)
                    body(pb + 1, 0, pb * R + R, True, False)
                with eng.Fori(1, R - 1) as r:
                    body(PAIRED - 1, r, r + (PAIRED - 1) * R, False, False)
                body(PAIRED - 1, R - 1, PAIRED * R - 1, False, True)

            block = ctx.enter_context(nc.Block())

            @block.tensor
            def _(pe):
                def gate(n, pb, r, q, first):
                    k = n // E
                    pe.wait_ge(pool_clo, q * ROWS + k + 1)
                    if first:
                        after(pe, dve_res, (pb - 1) * ROWS + k + 1)
                    for t in range(TILES):
                        last = nc.tensor.matmul(ps[6][:, t * E:(t + 1) * E], cur[k][:, t * P:(t + 1) * P],
                                                wg_sb[:, bass.ds(r * E, E)], start=True, stop=True)
                    last.then_inc(pe_gate, 1)

                def hidden(n, q):
                    k, e = divmod(n, E)
                    if isinstance(q, int) and q == 0 and k == 0:
                        if e in ACT_SPLITS:
                            pe.wait_ge(dve_wlo, 2 * ACT_SPLITS.index(e) + 1)
                        else:
                            pe.wait_ge(pool_wlo, 2 * POOL_SPLITS.index(e) + 1)
                    for c in range(FC):
                        after(pe, act_hid, q * (UNITS * FC) + (n - 1) * FC + c + 1)
                        w = slice(c * P, (c + 1) * P)
                        nc.tensor.matmul(ps[c][:, :], w1_hi[:, e, w], cur_hi[k][:, :], start=True, stop=False)
                        nc.tensor.matmul(ps[c][:, :], w1_hi[:, e, w], cur_lo[k][:, :], start=False, stop=False)
                        nc.tensor.matmul(ps[c][:, :], w1_lo[:, e, w], cur_hi[k][:, :], start=False, stop=True).then_inc(pe_hid, 1)
                        if e == 1 and c == 1:
                            turn_weights(n, q)

                def turn_weights(n, q):
                    k = n // E
                    pe.wait_ge(dve_gate, (q * ROWS + k) * GATE + GATE)
                    for t in range(TILES):
                        last = nc.tensor.transpose(ps[6][0:2 * E, t * P:(t + 1) * P], cw_hl[:, t, :], ident[:, :])
                    last.then_inc(pe_cwT, 1)

                def spread_weights(n, q):
                    k, e = divmod(n, E)
                    if e == 0:
                        pe.wait_ge(act_cwT, q * ROWS + k + 1)
                    after(pe, act_cwb, q * UNITS + n)
                    nc.tensor.matmul(ps[7][:, :], sel[:, e, :], cwT[:, :], start=True, stop=True).then_inc(pe_cwb, 1)

                def expert(n, q):
                    e = n % E
                    after(pe, dve_share, q * UNITS + n - 1)
                    if isinstance(q, int) and q == 0 and n < E:
                        if e in ACT_SPLITS:
                            pe.wait_ge(dve_wlo, 2 * ACT_SPLITS.index(e) + 2)
                        else:
                            pe.wait_ge(pool_wlo, 2 * POOL_SPLITS.index(e) + 2)
                    y = ps[4 + n % 2]
                    for c in range(FC):
                        pe.wait_ge(dve_lo, q * (UNITS * FC) + n * FC + c + 1)
                        last = nc.tensor.matmul(y[:, :], w2_hi[:, e, c, :], hid_hi[n % 2][:, c, :], start=(c == 0), stop=False)
                        last = nc.tensor.matmul(y[:, :], w2_hi[:, e, c, :], hid_lo[n % 2][:, c, :], start=False, stop=False)
                        last = nc.tensor.matmul(y[:, :], w2_lo[:, e, c, :], hid_hi[n % 2][:, c, :], start=False, stop=(c == FC - 1))
                    last.then_inc(pe_y, 1)

                def finish(k, pb):
                    pe.wait_ge(dve_fin, pb * ROWS + k + 1)
                    for t in range(TILES):
                        tok = slice(t * P, (t + 1) * P)
                        last = nc.tensor.transpose(ps[6][:, tok], fin[k][:, tok], ident[:, :])
                    last.then_inc(pe_fin, 1)

                def body(pb, r, q, first, last):
                    for n in range(UNITS):
                        if n % E == 0:
                            gate(n, pb, r, q, first)
                        if first and n == 2 and there(pb - 1):
                            pe.wait_ge(act_cwT, q * ROWS + 1)
                            finish(1, pb - 1)
                        if last and n == 7:
                            pe.wait_ge(act_cwT, q * ROWS + 2)
                            finish(0, pb)
                        hidden(n, q)
                        if n:
                            expert(n - 1, q)
                            spread_weights(n - 1, q)
                    expert(UNITS - 1, q)
                    spread_weights(UNITS - 1, q)

                pe.wait_ge(f_sel, 1)
                loops(pe, body)
                pe.wait_ge(dve_res, B - 1)
                finish(1, PAIRED - 1)

            @block.scalar
            def _(act):
                def gelus(n, q):
                    e = n % E
                    for c in range(FC):
                        g = q * (UNITS * FC) + n * FC + c
                        act.wait_ge(pe_hid, g + 1)
                        b1 = B1 + e * FC + c
                        nc.scalar.activation(hid[n % 2][:, c, :], ps[c][:, :], ACT.Gelu_apprx_tanh,
                                             bias=biasT[:, b1:b1 + 1]).then_inc(act_hid, 1)
                        if e == 0 and c == 2:
                            act.wait_ge(dve_gate, (q * ROWS + n // E) * GATE + 10)
                            nc.scalar.activation(th[:, :, :], gap[:, :, :], ACT.Tanh).then_inc(act_tanh, 1)
                        if e == 1 and c == 2:
                            copy_weights(n, q)

                def highs(n, q):
                    for c in (0, 1):
                        act.wait_ge(act_hid, q * (UNITS * FC) + n * FC + c + 1)
                        nc.scalar.copy(hid_hi[n % 2][:, c, :], hid[n % 2][:, c, :]).then_inc(act_hi, 1)

                def copy_weights(n, q):
                    act.wait_ge(pe_cwT, q * ROWS + n // E + 1)
                    nc.scalar.copy(cwT[:, :], ps[6][0:2 * E, :]).then_inc(act_cwT, 1)

                def copy_spread(n, q):
                    act.wait_ge(pe_cwb, q * UNITS + n + 1)
                    after(act, dve_share, q * UNITS + n - 1)
                    nc.scalar.copy(cwb[n % 2][:, :], ps[7][:, :]).then_inc(act_cwb, 1)

                def load(k, pb):
                    after(act, dve_fin, (pb - 1) * ROWS + k + 1)
                    nc.scalar.copy(cur[k][:, :], cur_all[:, bass.ds((pb * ROWS + k) * S, S)]).then_inc(act_cur, 1)

                def body(pb, r, q, first, last):
                    for n in range(UNITS):
                        if first and n == 2 and there(pb - 1):
                            load(1, pb)
                        if last and n == 7 and not isinstance(pb, int):
                            load(0, pb + 1)
                        gelus(n, q)
                        highs(n, q)
                        if n:
                            copy_spread(n - 1, q)
                    copy_spread(UNITS - 1, q)

                for k in range(ROWS):
                    load(k, 0)
                act.wait_ge(ld_ffn, 16 * (3 + TILES))
                for e in ACT_SPLITS:
                    nc.scalar.copy(w1_hi[:, e, :], w1_raw[:, e * F:(e + 1) * F]).then_inc(act_whi, 1)
                    w = slice(e * FC * D, (e + 1) * FC * D)
                    nc.scalar.copy(w2_hi[:, e, :, :], w2_raw[:, w].rearrange("p (c d) -> p c d", d=D)).then_inc(act_whi, 1)
                act.wait_ge(f_const, 6)
                nc.scalar.copy(sel[:, :, :], sel_f[:, :, :]).then_inc(f_sel, 1)
                loops(act, body)

            @block.vector
            def _(dve):
                def gates(n, r, q):
                    base = (q * ROWS + n // E) * GATE
                    by_j = logit[:, :, :].unsqueeze(2).to_broadcast([P, TILES, E, E])
                    by_e = logit[:, :, :].unsqueeze(3).to_broadcast([P, TILES, E, E])
                    dve.wait_ge(pe_gate, q * ROWS + n // E + 1)
                    nc.vector.tensor_tensor(logit[:, :, :], ps[6][:, 0:TILES * E].rearrange("p (t e) -> p t e", e=E),
                                            bg_sb[:, bass.ds(r, 1), :, :].rearrange("p r t e -> p (r t) e"), ALU.add).then_inc(dve_gate, 1)
                    dve.wait_ge(dve_gate, base + 1)
                    nc.vector.tensor_tensor(gt[:, :, :, :], by_j, by_e, ALU.is_gt).then_inc(dve_gate, 1)
                    nc.vector.tensor_tensor(eq[:, :, :, :], by_j, by_e, ALU.is_equal).then_inc(dve_gate, 1)
                    dve.wait_ge(dve_gate, base + 3)
                    nc.vector.tensor_tensor(eq[:, :, :, :], eq[:, :, :, :],
                                            earlier[:, :, :].unsqueeze(1).to_broadcast([P, TILES, E, E]), ALU.mult).then_inc(dve_gate, 1)
                    dve.wait_ge(dve_gate, base + 4)
                    nc.vector.tensor_tensor(gt[:, :, :, :], gt[:, :, :, :], eq[:, :, :, :], ALU.add).then_inc(dve_gate, 1)
                    dve.wait_ge(dve_gate, base + 5)
                    nc.vector.tensor_reduce(rank[:, :, :], gt[:, :, :, :], AX_X, ALU.add).then_inc(dve_gate, 1)
                    dve.wait_ge(dve_gate, base + 6)
                    nc.vector.tensor_scalar(chosen[:, :, :], rank[:, :, :], 2.0, None, ALU.is_lt).then_inc(dve_gate, 1)
                    dve.wait_ge(dve_gate, base + 7)
                    nc.vector.tensor_tensor(picked[:, :, :], logit[:, :, :], chosen[:, :, :], ALU.mult).then_inc(dve_gate, 1)
                    dve.wait_ge(dve_gate, base + 8)
                    nc.vector.tensor_reduce(pair_sum[:, :], picked[:, :, :], AX_X, ALU.add).then_inc(dve_gate, 1)
                    dve.wait_ge(dve_gate, base + 9)
                    nc.vector.scalar_tensor_tensor(out=gap[:, :, :], in0=pair_sum[:, :].unsqueeze(2).to_broadcast([P, TILES, E]),
                                                   scalar=-0.5, in1=logit[:, :, :], op0=ALU.mult, op1=ALU.add).then_inc(dve_gate, 1)

                def weights(n, q):
                    base = (q * ROWS + n // E) * GATE
                    dve.wait_ge(act_tanh, q * ROWS + n // E + 1)
                    nc.vector.scalar_tensor_tensor(out=cw2[:, :, :], in0=th[:, :, :], scalar=1.0, in1=chosen[:, :, :],
                                                   op0=ALU.add, op1=ALU.mult).then_inc(dve_gate, 1)
                    dve.wait_ge(dve_gate, base + 11)
                    nc.vector.tensor_scalar(cw_hl[:, :, 0:E].bitcast(F32R), cw2[:, :, :], 0.5, None, ALU.mult).then_inc(dve_gate, 1)
                    dve.wait_ge(dve_gate, base + 12)
                    nc.vector.scalar_tensor_tensor(out=cw_hl[:, :, E:2 * E], in0=cw2[:, :, :], scalar=0.5, in1=cw_hl[:, :, 0:E],
                                                   op0=ALU.mult, op1=ALU.subtract).then_inc(dve_gate, 1)

                def lows(n, q):
                    base = q * (UNITS * FC) + n * FC
                    for part, c in (("lo", 0), ("hi", 2), ("lo", 1), ("hi", 3), ("lo", 2), ("lo", 3)):
                        if part == "hi":
                            dve.wait_ge(act_hid, base + c + 1)
                            nc.vector.tensor_copy(hid_hi[n % 2][:, c, :], hid[n % 2][:, c, :]).then_inc(dve_hi, 1)
                            continue
                        if c < 2:
                            dve.wait_ge(act_hi, q * (UNITS * 2) + n * 2 + c + 1)
                        else:
                            dve.wait_ge(dve_hi, (q * UNITS + n) * 2 + c - 1)
                        nc.vector.tensor_tensor(hid_lo[n % 2][:, c, :], hid[n % 2][:, c, :], hid_hi[n % 2][:, c, :].bitcast(F32),
                                                ALU.subtract).then_inc(dve_lo, 1)

                def shares(n, q):
                    e = n % E
                    dve.wait_ge(pe_y, q * UNITS + n + 1)
                    dve.wait_ge(act_cwb, q * UNITS + n + 1)
                    after(dve, pool_cur, q * UNITS + n - 1)
                    nc.vector.scalar_tensor_tensor(out=share[n % 2][:, :], in0=ps[4 + n % 2][:, :], scalar=biasT[:, B2 + e:B2 + e + 1],
                                                   in1=cwb[n % 2][:, :], op0=ALU.add, op1=ALU.mult).then_inc(dve_share, 1)

                def finish(k, pb):
                    dve.wait_ge(pool_cur, (pb * R + R - 1) * UNITS + (k + 1) * E)
                    nc.vector.tensor_scalar(fin[k][:, :], cur[k][:, :], modT[:, 5, bass.ds(pb * ROWS + k, 1)], None,
                                            ALU.mult).then_inc(dve_fin, 1)

                def result(k, pb):
                    dve.wait_ge(pe_fin, pb * ROWS + k + 1)
                    xr = x_sb[:, bass.ds((pb * ROWS + k) * S, S)]
                    nc.vector.tensor_tensor(xr, ps[6][:, :], xr, ALU.add).then_inc(dve_res, 1)

                def body(pb, r, q, first, last):
                    for n in range(UNITS):
                        if n % E == 0:
                            gates(n, r, q)
                            weights(n, q)
                        lows(n, q)
                        if first and n == 0 and there(pb - 1):
                            finish(1, pb - 1)
                        if n:
                            shares(n - 1, q)
                        if first and n == 2 and there(pb - 1):
                            result(1, pb - 1)
                        if last:
                            if n == 5:
                                finish(0, pb)
                            if n == 7:
                                result(0, pb)
                    shares(UNITS - 1, q)

                for i, e in enumerate(ACT_SPLITS):
                    dve.wait_ge(act_whi, 2 * i + 1)
                    nc.vector.tensor_tensor(w1_lo[:, e, :], w1_raw[:, e * F:(e + 1) * F], w1_hi[:, e, :].bitcast(F32),
                                            ALU.subtract).then_inc(dve_wlo, 1)
                    dve.wait_ge(act_whi, 2 * i + 2)
                    w = slice(e * FC * D, (e + 1) * FC * D)
                    nc.vector.tensor_tensor(w2_lo[:, e, :, :], w2_raw[:, w].rearrange("p (c d) -> p c d", d=D),
                                            w2_hi[:, e, :, :].bitcast(F32), ALU.subtract).then_inc(dve_wlo, 1)
                dve.wait_ge(f_const, 6)
                loops(dve, body)
                finish(1, PAIRED - 1)
                result(1, PAIRED - 1)

            @block.gpsimd
            def _(pool):
                def split(k, q):
                    pool.sem_inc(pool_waited, 1)
                    nc.gpsimd.tensor_scalar(cur_hi[k][:, :], cur[k][:, :], 1.0, 1.0, ALU.mult, ALU.mult).then_inc(pool_chi, 1)
                    pool.wait_ge(pool_chi, q * ROWS + k + 1)
                    nc.gpsimd.tensor_tensor(cur_lo[k][:, :], cur[k][:, :], cur_hi[k][:, :].bitcast(F32), ALU.subtract).then_inc(pool_clo, 1)

                def add(n, pb, q, last):
                    k, e = divmod(n, E)
                    pool.wait_ge(dve_share, q * UNITS + n + 1)
                    after(pool, pool_cur, q * UNITS + n)
                    nc.gpsimd.tensor_tensor(cur[k][:, :], cur[k][:, :], share[n % 2][:, :], ALU.add).then_inc(pool_cur, 1)
                    if e == E - 1 and not last:
                        pool.wait_ge(pool_cur, q * UNITS + n + 1)
                        split(k, q + 1)

                def split_new(k, pb):
                    pool.wait_ge(act_cur, pb * ROWS + k + 1)
                    split(k, pb * R)

                def body(pb, r, q, first, last):
                    for n in range(UNITS):
                        if first and n == 0 and there(pb - 1):
                            split_new(1, pb)
                        add(n, pb, q, last)
                        if last and n == 5 and not isinstance(pb, int):
                            split_new(0, pb + 1)

                def split_weights(raw, hi, lo, count):
                    nc.gpsimd.tensor_scalar(hi, raw, 1.0, 1.0, ALU.mult, ALU.mult).then_inc(pool_whi, 1)
                    pool.wait_ge(pool_whi, count)
                    nc.gpsimd.tensor_tensor(lo, raw, hi.bitcast(F32), ALU.subtract).then_inc(pool_wlo, 1)

                for k in range(ROWS):
                    split_new(k, 0)
                nc.gpsimd.memset(earlier[:, :, :], 1.0).then_inc(f_const, 1)
                nc.gpsimd.memset(sel_f[:, :, :], 0.0).then_inc(f_const, 1)
                pool.wait_ge(f_const, 2)
                nc.gpsimd.affine_select(out=earlier[:, :, :], in_=earlier[:, :, :], compare_op=ALU.is_gt, fill=0.0, base=0,
                                        pattern=[[1, E], [-1, E]], channel_multiplier=0).then_inc(f_const, 1)
                nc.gpsimd.affine_select(out=sel_f[:, :, :], in_=sel_f[:, :, :], compare_op=ALU.not_equal, fill=1.0, base=0,
                                        pattern=[[-1, E], [0, P]], channel_multiplier=1).then_inc(f_const, 1)
                pool.wait_ge(f_const, 4)
                nc.gpsimd.affine_select(out=sel_f[:, :, :], in_=sel_f[:, :, :], compare_op=ALU.not_equal, fill=1.0, base=-E,
                                        pattern=[[-1, E], [0, P]], channel_multiplier=1).then_inc(f_const, 2)
                pool.wait_ge(ld_ffn, 16 * (3 + TILES))
                for i, e in enumerate(POOL_SPLITS):
                    w = slice(e * F, (e + 1) * F)
                    split_weights(w1_raw[:, w], w1_hi[:, e, :], w1_lo[:, e, :], 2 * i + 1)
                    split_weights(w2_raw[:, w], w2_hi[:, e, :, :].rearrange("p c d -> p (c d)"),
                                  w2_lo[:, e, :, :].rearrange("p c d -> p (c d)"), 2 * i + 2)
                loops(pool, body)

            @block.sync
            def _(sp):
                out_v = out.rearrange("b (t p) d -> b p t d", p=P)
                with sp.Fori(0, B) as row:
                    sp.wait_ge(dve_res, row + 1)
                    sp.dma_start(out_v[bass.ds(row, 1)].rearrange("b p t d -> p (b t) d"),
                                 x_sb[:, bass.ds(row * S, S)].rearrange("p (t d) -> p t d", d=D)).then_inc(stored, 16)
                sp.wait_ge(stored, 16 * B)


_INS = ["L0_attn_x", "L0_attn_Q_w", "L0_attn_Q_b", "L0_attn_K_w", "L0_attn_K_b", "L0_attn_V_w", "L0_attn_V_b", "L0_attn_O_w",
        "L0_attn_O_b", "L0_ffn_Wg", "L0_ffn_bg", "L0_ffn_W1", "L0_ffn_b1", "L0_ffn_W2", "L0_ffn_b2", "L0_c", "L0_wmod"]


def kernel(**inputs):
    import numpy as np
    import concourse.bacc as bacc
    from concourse.bass_utils import run_bass_kernel_spmd

    nc = bacc.Bacc("TRN2", target_bir_lowering=False, num_devices=1)
    arrays, args = {}, []
    for name in _INS:
        a = np.ascontiguousarray(inputs[name])
        arrays["in_" + name] = a
        args.append(nc.dram_tensor("in_" + name, a.shape, mybir.dt.from_np(a.dtype), kind="ExternalInput").ap())
    out = nc.dram_tensor("out_x", inputs["L0_attn_x"].shape, F32, kind="ExternalOutput").ap()
    adaln_block(nc, args, out)
    r = run_bass_kernel_spmd(nc, [arrays], core_ids=[0])
    return r.results[0]["out_x"]
```

```python
from contextlib import ExitStack

import concourse.bass as bass
from concourse import mybir
from concourse.alu_op_type import AluOpType as ALU

ACT = mybir.ActivationFunctionType
F32 = mybir.dt.float32
F32R = mybir.dt.float32r
AX_X = mybir.AxisListType.X

P = 128
EPS = 1e-5
NEG = -1.0e30
BIG = 3.0e38




def adaln_block(nc, ins, out):
    x_d, qw_d, qb_d, kw_d, kb_d, vw_d, vb_d, ow_d, ob_d, wg_d, bg_d, w1_d, b1_d, w2_d, b2_d, c_d, wmod_d = ins
    B, S, D = x_d.shape
    H, _, DH = qw_d.shape
    R, _, E = wg_d.shape
    F = w1_d.shape[2]
    TILES = S // P
    PAIRS = H // 2
    FC = F // P
    SCALE = float(DH) ** -0.5
    assert D == P and DH == 64 and S == 512 and TILES == 4 and H == 16 and E == 4

    P_OFF = [P * (i * (i + 1) // 2) for i in range(TILES + 1)]
    P_COLS = P_OFF[TILES]
    PT_OFF = [0, 512, 1152, 896]
    PT_DATA3 = 1024
    PT_COLS = 1408
    CHUNKS = [
        ([(i, 0) for i in range(4)], 0),
        ([(i, 1) for i in range(1, 4)], 512),
        ([(3, 3), (2, 2), (3, 2)], PT_DATA3),
    ]

    ITEMS = [
        [("q", 2, 0), ("v", 3, 0)],
        [("k", 2, 0)],
        [("q", 3, 0)],
        [("k", 3, 0)],
        [("k", 4, 0), ("q", 4, 0)],
        [("v", 4, 0), ("v", 5, 0)],
        [("v", 6, 0), ("q", 5, 0)],
        [("k", 5, 0)],
        [("v", 7, 0), ("q", 6, 0)],
        [("k", 6, 0), ("h2", 0, -1)],
        [("q", 7, 0), ("k", 7, 0)],
        [],
        [("h", 0, 1)],
        [("q", 0, 1), ("k", 0, 1)],
        [("v", 0, 1), ("v", 1, 1)],
        [("k", 1, 1), ("q", 1, 1), ("v", 2, 1)],
    ]
    ORDER = {
        "pe": (
            [("items", 0), ("scores", 0), ("scores", 1), ("turn", 0), ("turn", 1), ("items", 1), ("values", 0),
             ("scores", 2), ("scores", 3), ("turn", 2), ("project", 0)],
            [("items", 0), ("scores", 0), ("scores", 1), ("turn", 0), ("turn", 1), ("items", 1), ("values", 0),
             ("scores", 2), ("scores", 3), ("turn", 2), ("project", 0)],
        ),
        "act": (
            [("items", 0), ("turn", 0), ("items", 1), ("scores", 0), ("turn", 1), ("scores", 1), ("values", 0),
             ("turn", 2), ("scores", 2), ("scores", 3)],
            [("items", 0), ("turn", 0), ("items", 1), ("turn", 1), ("scores", 0), ("scores", 1), ("values", 0),
             ("turn", 2), ("scores", 2), ("scores", 3)],
        ),
        "dve": (
            [("scores", 0), ("scores", 1), ("inverse", 0), ("items", 0), ("turn", 0), ("items", 1), ("scores", 2),
             ("scores", 3), ("turn", 1), ("turn", 2)],
            [("scores", 0), ("inverse", 0), ("scores", 1), ("items", 0), ("turn", 0), ("items", 1), ("scores", 2),
             ("scores", 3), ("turn", 1), ("turn", 2)],
        ),
    }
    AT = {
        "project6": 0, "project7": 2, "gate": 3, "add": 4, "moments2": 4,
        "root2": 7, "normal2": 7, "moments1": 8, "root1": 9, "normal1": 10,
    }
    DVE_V = [0, 2]
    FLAT = [(step, item) for step in range(H) for item in ITEMS[step]]
    assert len(FLAT) % 2 == 0
    H_STEP = next(step for step, item in FLAT if item[0] == "h")

    def there(b):
        return not isinstance(b, int) or 0 <= b < B

    with ExitStack() as whole:
        def sb(ctx, name, shape, dt=F32):
            return ctx.enter_context(nc.sbuf_tensor(name, shape, dt))

        def sem(name):
            return whole.enter_context(nc.semaphore(name))

        x_sb = sb(whole, "x_sb", [P, B * TILES * D])
        cur_all = sb(whole, "cur_all", [P, B * S])
        w1_raw = sb(whole, "w1_raw", [P, E * F])
        w2_raw = sb(whole, "w2_raw", [P, E * FC * D])
        ident = sb(whole, "ident", [P, P])
        modT = sb(whole, "modT", [P, 6, B])
        biasT = sb(whole, "biasT", [P, 40])
        wg_sb = sb(whole, "wg_sb", [P, R * E])
        bg_sb = sb(whole, "bg_sb", [P, R, TILES, E])
        NB1 = E * FC
        QB, KB, B1, B2, OB = 0, PAIRS, 2 * PAIRS, 2 * PAIRS + NB1, 2 * PAIRS + NB1 + E
        NROWS = OB + 1

        earlier = sb(whole, "earlier", [P, E, E])

        ps = [whole.enter_context(nc.psum_tensor(f"bank{i}", [P, 512], F32)) for i in range(8)]

        dve_waited = sem("dve_waited")
        pool_waited = sem("pool_waited")

        ld_c = sem("ld_c")
        ld_bias = sem("ld_bias")
        ld_wmod = sem("ld_wmod")
        ld_x = [sem(f"ld_x{i}") for i in range(2)]
        ld_w = {n: sem("ld_" + n) for n in ("wq", "wk", "wv", "wo")}
        ld_ffn = sem("ld_ffn")

        w_names = ["wq", "wk", "wv", "wo"]
        w_hi = {"wo": sb(whole, "wo_hi", [P, H * DH], F32R)}
        w_lo = {"wo": sb(whole, "wo_lo", [P, H * DH], F32R)}
        norm2 = sb(whole, "norm2", [P, TILES * D])
        gated = sb(whole, "gated", [P, S])
        att = [sb(whole, f"att{i}", [P, S]) for i in range(2)]
        att_of_lo = [sb(whole, f"att_of_lo{i}", [P, S]) for i in range(2)]
        att_hi = [sb(whole, f"att_hi{i}", [P, S], F32R) for i in range(2)]
        att_lo = [sb(whole, f"att_lo{i}", [P, S], F32R) for i in range(2)]
        bn2 = sb(whole, "bn2", [P, TILES, 6])
        mv2 = sb(whole, "mv2", [P, TILES, 2])
        ve2 = sb(whole, "ve2", [P, TILES])
        rstd2 = sb(whole, "rstd2", [P, TILES])
        minus_half = sb(whole, "minus_half", [P, TILES])
        vbT = sb(whole, "vbT", [DH, H])

        with ExitStack() as ctx:
            for n in ("wq", "wk", "wv"):
                w_hi[n] = sb(ctx, n + "_hi", [P, H * DH], F32R)
                w_lo[n] = sb(ctx, n + "_lo", [P, H * DH], F32R)
            v_hl = [sb(ctx, f"v_hl{i}", [P, TILES, H // 2, 2 * DH], F32R) for i in range(2)]
            prob = sb(ctx, "prob", [P, 4, P_COLS])
            neg_s = sb(ctx, "neg_s", [P, P_COLS])
            pt_hi = [sb(ctx, f"pt_hi{i}", [P, PT_COLS], F32R) for i in range(2)]
            pt_lo = [sb(ctx, f"pt_lo{i}", [P, PT_COLS], F32R) for i in range(2)]
            q_hi = [sb(ctx, f"q_hi{i}", [P, S], F32R) for i in range(2)]
            q_lo = [sb(ctx, f"q_lo{i}", [P, S], F32R) for i in range(2)]
            k_hi = [sb(ctx, f"k_hi{i}", [P, S], F32R) for i in range(2)]
            k_lo = [sb(ctx, f"k_lo{i}", [P, S], F32R) for i in range(2)]
            h_f = gated
            h_hi = sb(ctx, "h_hi", [P, S], F32R)
            h_lo = sb(ctx, "h_lo", [P, S], F32R)
            norm1 = sb(ctx, "norm1", [P, TILES * D])
            mask = sb(ctx, "mask", [P, S])
            negmax = sb(ctx, "negmax", [P, TILES])
            sums = sb(ctx, "sums", [P, 4, TILES])
            rinv = sb(ctx, "rinv", [P, 4, TILES])
            bn1 = sb(ctx, "bn1", [P, TILES, 6])
            mv1 = sb(ctx, "mv1", [P, TILES, 2])
            ve1 = sb(ctx, "ve1", [P, TILES])
            rstd1 = sb(ctx, "rstd1", [P, TILES])
            raw = {n: prob[:, i, 0:H * DH] for i, n in enumerate(w_names)}
            wmod_raw = cur_all[:, 0:6 * D]
            c_sb = cur_all[0:B, 1024:1024 + D]
            c_act = cur_all[0:B, 1152:1152 + D]
            c_tanh = cur_all[0:B, 1280:1280 + D]
            siluT = cur_all[:, 1408:1408 + B]
            rows = cur_all[0:NROWS, 1536:1536 + P]
            vb_rows = cur_all[0:H, 1664:1664 + DH]
            ga_pos = cur_all[:, 1792:1792 + 2 * B]
            ga_neg = cur_all[:, 1856:1856 + 2 * B]

        su_const = sem("su_const")
        su_tanh = sem("su_tanh")
        su_dve = sem("su_dve")
        su_pe = sem("su_pe")
        f_const = sem("f_const")
        su_whi = sem("su_whi")
        dve_wlo = sem("dve_wlo")
        pool_wlo = sem("pool_wlo")
        pe_item = {n: sem("pe_" + n) for n in ("q", "k", "v", "h", "h2")}
        pe_s = sem("pe_s")
        pe_t = sem("pe_t")
        pe_pv = sem("pe_pv")
        pe_o = sem("pe_o")
        pe_yt = sem("pe_yt")
        act_item = {n: sem("act_" + n) for n in ("q", "k", "v", "h")}
        act_exp = sem("act_exp")
        act_pt = sem("act_pt")
        act_att = sem("act_att")
        dve_item = {n: sem("dve_" + n) for n in ("q", "k", "v", "h", "h2")}
        dve_vhi = sem("dve_vhi")
        dve_min = sem("dve_min")
        dve_pt = sem("dve_pt")
        dve_rinv = sem("dve_rinv")
        dve_y = sem("dve_y")
        dve_x1 = sem("dve_x1")
        dve_bn1 = sem("dve_bn1")
        dve_bn2 = sem("dve_bn2")
        dve_ve1 = sem("dve_ve1")
        dve_ve2 = sem("dve_ve2")
        dve_norm1 = sem("dve_norm1")
        dve_norm2 = sem("dve_norm2")
        pool_hlo = sem("pool_hlo")
        pool_prob = sem("pool_prob")
        pool_att = sem("pool_att")
        pool_ahi = sem("pool_ahi")
        pool_alo = sem("pool_alo")
        pool_rstd1 = sem("pool_rstd1")
        pool_rstd2 = sem("pool_rstd2")

        def after(eng, s, n):
            if not isinstance(n, int) or n > 0:
                eng.wait_ge(s, n)

        def nth(kind, index, b):
            per_row = {"q": PAIRS, "k": PAIRS, "v": 2 * TILES, "h": 1, "h2": 1}[kind]
            return b * per_row + index + 1

        def bank_of(n):
            return ps[n % 2]

        def bank_free(eng, n, b):
            back = n - 2
            while True:
                step, (kind, index, rel) = FLAT[back % len(FLAT)]
                row = b + rel + (back // len(FLAT))
                if there(row):
                    break
                back -= 2
                if back < -2 * len(FLAT):
                    return
            after(eng, dve_item[kind], nth(kind, index, row))

        first = {}
        for n, (step, item) in enumerate(FLAT):
            first.setdefault(step, n)

        def items(b, u):
            return [(first[u] + i, kind, index, b + rel)
                    for i, (kind, index, rel) in enumerate(ITEMS[u]) if there(b + rel)]

        def scored(b, u):
            return (b, u + 2) if u + 2 < H else (b + 1, u + 2 - H)

        def scored_before(b, u):
            return (b, u + 1) if u + 1 < H else (b + 1, 0)

        def weighted(b, u):
            return (b, u - 1) if u else (b - 1, H - 1)

        ROWS = 2
        UNITS = ROWS * E
        PAIRED = B // ROWS
        ACT_SPLITS, POOL_SPLITS = (0, 1), (2, 3)
        assert E == 4 and PAIRED * ROWS == B and R > 2
        with ExitStack() as ctx:
            w1_hi = sb(ctx, "w1_hi", [P, E, F], F32R)
            w1_lo = sb(ctx, "w1_lo", [P, E, F], F32R)
            w2_hi = sb(ctx, "w2_hi", [P, E, FC, D], F32R)
            w2_lo = sb(ctx, "w2_lo", [P, E, FC, D], F32R)
            cur = [sb(ctx, f"cur{k}", [P, S]) for k in range(ROWS)]
            cur_hi = [sb(ctx, f"cur_hi{k}", [P, S], F32R) for k in range(ROWS)]
            cur_lo = [sb(ctx, f"cur_lo{k}", [P, S], F32R) for k in range(ROWS)]
            hid = [sb(ctx, f"hid{i}", [P, FC, S]) for i in range(2)]
            hid_hi = [sb(ctx, f"hid_hi{i}", [P, FC, S], F32R) for i in range(2)]
            hid_lo = [sb(ctx, f"hid_lo{i}", [P, FC, S], F32R) for i in range(2)]
            cwb = [sb(ctx, f"cwb{k}", [P, E, S]) for k in range(ROWS)]
            share = [sb(ctx, f"share{i}", [P, S]) for i in range(2)]
            logit = sb(ctx, "logit", [P, TILES, E])
            gt = sb(ctx, "gt", [P, TILES, E, E])
            eq = sb(ctx, "eq", [P, TILES, E, E])
            rank = sb(ctx, "rank", [P, TILES, E])
            chosen = sb(ctx, "chosen", [P, TILES, E])
            picked = sb(ctx, "picked", [P, TILES, E])
            pair_sum = sb(ctx, "pair_sum", [P, TILES])
            gap = sb(ctx, "gap", [P, TILES, E])
            th = sb(ctx, "th", [P, TILES, E])
            cw2 = sb(ctx, "cw2", [P, TILES, E])
            cwT = [sb(ctx, f"cwT{k}", [E, S]) for k in range(ROWS)]
            fin = [sb(ctx, f"fin{k}", [P, S]) for k in range(ROWS)]

        ffn_act_whi = sem("ffn_act_whi")
        ffn_dve_wlo = sem("ffn_dve_wlo")
        ffn_pool_whi = sem("ffn_pool_whi")
        ffn_pool_wlo = sem("ffn_pool_wlo")
        pe_hid = sem("pe_hid")
        pe_y = sem("pe_y")
        pe_gate = sem("pe_gate")
        pe_cwT = sem("pe_cwT")
        pe_fin = sem("pe_fin")
        act_hid = sem("act_hid")
        act_hi = sem("act_hi")
        act_tanh = sem("act_tanh")
        act_cwT = sem("act_cwT")
        act_cur = sem("act_cur")
        dve_hi = sem("dve_hi")
        dve_lo = sem("dve_lo")
        dve_gate = sem("dve_gate")
        dve_share = sem("dve_share")
        dve_fin = sem("dve_fin")
        dve_res = sem("dve_res")
        pool_cur = sem("pool_cur")
        act_chi = sem("act_chi")
        dve_clo = sem("dve_clo")
        pool_chi = sem("pool_chi")
        pool_clo = sem("pool_clo")
        cw_dram = nc.dram_tensor("expert_weights", (ROWS, E, S), F32, kind="Internal").ap()
        cw_out = sem("cw_out")
        cw_in = [[sem(f"cw_in{k}{e}") for e in range(E)] for k in range(ROWS)]
        stored = sem("stored")

        SHARES = [[], [], [0, 1], [2], [3], [], [4, 5], [6]]
        GATE = 11

        def loops(eng, body):
            body(0, 0, 0, True, False)
            with eng.Fori(0, PAIRED - 1) as pb:
                with eng.Fori(1, R - 1) as r:
                    body(pb, r, pb * R + r, False, False)
                body(pb, R - 1, pb * R + R - 1, False, True)
                body(pb + 1, 0, pb * R + R, True, False)
            with eng.Fori(1, R - 1) as r:
                body(PAIRED - 1, r, r + (PAIRED - 1) * R, False, False)
            body(PAIRED - 1, R - 1, PAIRED * R - 1, False, True)

        block = whole.enter_context(nc.Block())

        @block.sync
        def _(sp):
            sp.dma_start(c_sb, c_d).then_inc(ld_c, 16)
            xv = x_d.rearrange("b (t p) d -> p (b t) d", p=P)
            xs = x_sb[:, :].rearrange("p (n d) -> p n d", d=D)
            sp.dma_start(xs[:, 0:TILES, :], xv[:, 0:TILES, :]).then_inc(ld_x[0], 16)

            def load_weights(n, d):
                sp.dma_start(raw[n].rearrange("p (h d) -> p h d", d=DH), d.rearrange("h m d -> m h d")).then_inc(ld_w[n], 16)

            load_weights("wq", qw_d)
            load_weights("wk", kw_d)
            sp.dma_start(rows[QB:QB + PAIRS, :], qb_d.rearrange("(n two) d -> n (two d)", two=2)).then_inc(ld_bias, 16)
            sp.dma_start(rows[KB:KB + PAIRS, :], kb_d.rearrange("(n two) d -> n (two d)", two=2)).then_inc(ld_bias, 16)
            sp.dma_start(rows[B1:B1 + NB1, :], b1_d.rearrange("e (c f) -> (e c) f", f=P)).then_inc(ld_bias, 16)
            sp.dma_start(rows[B2:B2 + E, :], b2_d).then_inc(ld_bias, 16)
            sp.dma_start(rows[OB:OB + 1, :], ob_d.rearrange("(a m) -> a m", a=1)).then_inc(ld_bias, 16)
            sp.dma_start(vb_rows, vb_d).then_inc(ld_bias, 16)
            load_weights("wv", vw_d)
            sp.dma_start(raw["wo"].rearrange("p (n m) -> p n m", m=D),
                         ow_d.rearrange("(n two) d m -> (two d) n m", two=2)).then_inc(ld_w["wo"], 16)
            sp.dma_start(xs[:, TILES:, :], xv[:, TILES:, :]).then_inc(ld_x[1], 16)
            sp.dma_start(w1_raw[:, :].rearrange("p (e f) -> p e f", e=E), w1_d.rearrange("e h f -> h e f")).then_inc(ld_ffn, 16)
            sp.dma_start(w2_raw[:, :].rearrange("p (e c h) -> p e c h", e=E, c=FC),
                         w2_d.rearrange("e (c p) h -> p e c h", p=P)).then_inc(ld_ffn, 16)
            sp.dma_start(wg_sb[:, :].rearrange("p (r e) -> p r e", r=R), wg_d.rearrange("r h e -> h r e")).then_inc(ld_ffn, 16)
            for t in range(TILES):
                sp.dma_start(bg_sb[:, :, t, :], bg_d.partition_broadcast(P)).then_inc(ld_ffn, 16)

            out_v = out.rearrange("b (t p) d -> b p t d", p=P)

            def spread(k, q):
                sp.wait_ge(act_cwT, q * ROWS + k + 1)
                sp.dma_start(cw_dram[k], cwT[k][:, :]).then_inc(cw_out, 16)
                sp.wait_ge(cw_out, (q * ROWS + k) * 16 + 16)
                for e in range(E):
                    sp.dma_start(cwb[k][:, e, :], cw_dram[k, e].partition_broadcast(P)).then_inc(cw_in[k][e], 16)

            def store(k, pb):
                row = pb * ROWS + k
                sp.wait_ge(dve_res, row + 1)
                sp.dma_start(out_v[bass.ds(row, 1)].rearrange("b p t d -> p (b t) d"),
                             x_sb[:, bass.ds(row * S, S)].rearrange("p (t d) -> p t d", d=D)).then_inc(stored, 16)

            def body(pb, r, q, first, last):
                spread(0, q)
                if first and there(pb - 1):
                    store(1, pb - 1)
                spread(1, q)
                if last:
                    store(0, pb)

            loops(sp, body)
            store(1, PAIRED - 1)
            sp.wait_ge(stored, 16 * B)

        @block.tensor
        def _(pe):
            def three(out_ap, lhs_hi, lhs_lo, rhs_hi, rhs_lo, start=True, stop=True):
                nc.tensor.matmul(out_ap, lhs_hi, rhs_hi, start=start, stop=False)
                nc.tensor.matmul(out_ap, lhs_hi, rhs_lo, start=False, stop=False)
                return nc.tensor.matmul(out_ap, lhs_lo, rhs_hi, start=False, stop=stop)

            pe.wait_ge(su_const, 4)
            pe.wait_ge(su_dve, 1)
            nc.tensor.transpose(ps[2][:, 128:128 + B], c_act, ident[0:B, 0:B]).then_inc(su_pe, 1)
            pe.wait_ge(su_dve, 2)
            pe.wait_ge(ld_wmod, 16)
            for j in range(6):
                last = nc.tensor.matmul(ps[3][:, j * B:(j + 1) * B], wmod_raw[:, j * D:(j + 1) * D], siluT, start=True, stop=True)
            last.then_inc(su_pe, 1)

            def item(b, n, kind, index, row):
                bank_free(pe, n, b)
                bank = bank_of(n)
                if kind in ("q", "k", "v") and index == 0 and isinstance(row, int) and row == 0:
                    pe.wait_ge(pool_wlo if kind == "v" else dve_wlo, 2 if kind == "k" else 1)
                if kind in ("q", "k"):
                    if kind == "q" and index == 0:
                        pe.wait_ge(pool_hlo, row + 1)
                    w = slice(index * P, (index + 1) * P)
                    name = "w" + kind
                    three(bank[:, :], w_hi[name][:, w], w_lo[name][:, w], h_hi[:, :], h_lo[:, :]).then_inc(pe_item[kind], 1)
                if kind == "v":
                    half, t = divmod(index, TILES)
                    tok, cols = slice(t * P, (t + 1) * P), slice(half * 512, (half + 1) * 512)
                    three(bank[:, :], h_hi[:, tok], h_lo[:, tok], w_hi["wv"][:, cols], w_lo["wv"][:, cols]).then_inc(pe_item[kind], 1)
                if kind in ("h", "h2"):
                    turn_normal(kind, row, bank)

            def scores(b, u, i):
                pair, lo = u // 2, DH * (u % 2)
                half = slice(lo, lo + DH)
                if u % 2 == 0 and i == 0:
                    after(pe, dve_item["q"], nth("q", pair, b))
                    after(pe, dve_item["k"], nth("k", pair, b))
                after(pe, dve_min, (b * H + u) * TILES + i - 1)
                tok, keys = slice(i * P, (i + 1) * P), slice(0, max(256, (i + 1) * P))
                three(ps[2 + i % 2][:, keys], q_hi[pair % 2][half, tok], q_lo[pair % 2][half, tok],
                      k_hi[pair % 2][half, keys], k_lo[pair % 2][half, keys]).then_inc(pe_s, 1)

            def values(b, u):
                pair = u // 2
                if u % (H // 2) == 0:
                    after(pe, dve_item["v"], nth("v", TILES * (u * 2 // H) + TILES - 1, b))
                after(pe, dve_pt, (b * H + u) * 3 + 3)
                after(pe, act_att, b * H + u)
                for j in (0, 1, 2, 3):
                    width = max(256, S - j * P)
                    stat = v_hl[u * 2 // H][:, j, u % (H // 2), :]
                    cols = slice(PT_OFF[j], PT_OFF[j] + width)
                    for n, part in enumerate((pt_hi, pt_lo)):
                        last = nc.tensor.matmul(ps[6][:, S - width:S], stat, part[u % 2][:, cols],
                                                start=(j == 0 and n == 0), stop=(j == 3 and n == 1))
                last.then_inc(pe_pv, 1)

            def turn(b, u, c):
                if c == 0:
                    after(pe, pool_prob, b * H + u + 1)
                after(pe, dve_pt, (b * H + u) * 3 + c - 1)
                bank = ps[4 + (u * 3 + c) % 2]
                for z, (i, j) in enumerate(CHUNKS[c][0]):
                    col = P_OFF[i] + j * P
                    last = nc.tensor.transpose(bank[:, z * P:(z + 1) * P], prob[:, u % 4, col:col + P], ident[:, :])
                last.then_inc(pe_t, 1)

            def project(b, pair):
                after(pe, pool_alo, b * PAIRS + pair + 1)
                if pair == 0:
                    after(pe, dve_x1, b)
                    if isinstance(b, int) and b == 0:
                        pe.wait_ge(pool_wlo, 2)
                w = slice(pair * D, (pair + 1) * D)
                three(ps[7][:, :], w_hi["wo"][:, w], w_lo["wo"][:, w], att_hi[pair % 2][:, :], att_lo[pair % 2][:, :],
                      start=(pair == 0), stop=(pair == PAIRS - 1)).then_inc(pe_o, 1)

            def turn_gated(row):
                after(pe, dve_y, row + 1)
                for t in range(TILES):
                    tok = slice(t * P, (t + 1) * P)
                    last = nc.tensor.transpose(ps[7][:, tok], gated[:, tok], ident[:, :])
                last.then_inc(pe_yt, 1)

            def turn_normal(kind, row, bank):
                after(pe, dve_norm1 if kind == "h" else dve_norm2, row + 1)
                src = norm1 if kind == "h" else norm2
                for t in range(TILES):
                    tok = slice(t * P, (t + 1) * P)
                    last = nc.tensor.transpose(bank[:, tok], src[:, tok], ident[:, :])
                last.then_inc(pe_item[kind], 1)

            def step(b, u):
                if u == AT["add"] and there(b - 1):
                    turn_gated(b - 1)
                todo = items(b, u)
                for part, i in ORDER["pe"][u % 2]:
                    if part == "scores" and there(scored(b, u)[0]):
                        scores(*scored(b, u), i)
                    if part == "turn" and there(b):
                        turn(b, u, i)
                    if part == "values" and there(weighted(b, u)[0]):
                        values(*weighted(b, u))
                    if part == "items":
                        for what in (todo[1:] if i else todo[:1]):
                            item(b, *what)
                    if part == "project":
                        if u == AT["project6"] and there(b - 1):
                            project(b - 1, PAIRS - 2)
                        if u == AT["project7"] and there(b - 1):
                            project(b - 1, PAIRS - 1)
                        if u >= 4 and u % 2 == 0 and there(b):
                            project(b, (u - 4) // 2)

            for u in range(8, H_STEP + 1):
                step(-1, u)
            pe.wait_ge(ld_bias, 16 * 6)
            nc.tensor.transpose(ps[2][:, 0:NROWS], rows, ident[0:NROWS, 0:NROWS])
            nc.tensor.transpose(ps[2][0:DH, 64:64 + H], vb_rows, ident[0:H, 0:H]).then_inc(su_pe, 1)
            for u in range(H_STEP + 1, H):
                step(-1, u)
            for u in range(H):
                step(0, u)
            with pe.Fori(1, B - 1) as b:
                for u in range(H):
                    step(b, u)
            for u in range(H):
                step(B - 1, u)
            step(B, 0)

            def gate(n, pb, r, q, first):
                k = n // E
                if isinstance(q, int) and q == 0 and k == 0:
                    pe.wait_ge(act_cur, 1)
                else:
                    pe.wait_ge(pool_clo, q * ROWS + k)
                if first:
                    after(pe, dve_res, (pb - 1) * ROWS + k + 1)
                for t in range(TILES):
                    last = nc.tensor.matmul(ps[6][:, t * E:(t + 1) * E], cur[k][:, t * P:(t + 1) * P],
                                            wg_sb[:, bass.ds(r * E, E)], start=True, stop=True)
                last.then_inc(pe_gate, 1)

            def hidden(n, q):
                k, e = divmod(n, E)
                if isinstance(q, int) and q == 0 and k == 0:
                    pe.wait_ge(dve_clo, 1)
                    if e in ACT_SPLITS:
                        pe.wait_ge(ffn_dve_wlo, ACT_SPLITS.index(e) + 1)
                    else:
                        pe.wait_ge(ffn_pool_wlo, 2 * POOL_SPLITS.index(e) + 1)
                for c in range(FC):
                    after(pe, act_hid, q * (UNITS * FC) + (n - 1) * FC + c + 1)
                    w = slice(c * P, (c + 1) * P)
                    nc.tensor.matmul(ps[c][:, :], w1_hi[:, e, w], cur_hi[k][:, :], start=True, stop=False)
                    nc.tensor.matmul(ps[c][:, :], w1_hi[:, e, w], cur_lo[k][:, :], start=False, stop=False)
                    nc.tensor.matmul(ps[c][:, :], w1_lo[:, e, w], cur_hi[k][:, :], start=False, stop=True).then_inc(pe_hid, 1)
                    if e == 1 and c == 1:
                        turn_weights(n, q)

            def turn_weights(n, q):
                k = n // E
                pe.wait_ge(dve_gate, (q * ROWS + k) * GATE + GATE)
                for t in range(TILES):
                    last = nc.tensor.transpose(ps[6][0:E, t * P:(t + 1) * P], cw2[:, t, :], ident[:, :])
                last.then_inc(pe_cwT, 1)

            def expert(n, q):
                e = n % E
                after(pe, dve_share, q * UNITS + n - 1)
                if isinstance(q, int) and q == 0 and n < E:
                    if e in ACT_SPLITS:
                        pe.wait_ge(ffn_dve_wlo, len(ACT_SPLITS) + ACT_SPLITS.index(e) + 1)
                    else:
                        pe.wait_ge(ffn_pool_wlo, 2 * POOL_SPLITS.index(e) + 2)
                y = ps[4 + n % 2]
                for c in range(FC):
                    pe.wait_ge(dve_lo, q * (UNITS * FC) + n * FC + c + 1)
                    last = nc.tensor.matmul(y[:, :], w2_hi[:, e, c, :], hid_hi[n % 2][:, c, :], start=(c == 0), stop=False)
                    last = nc.tensor.matmul(y[:, :], w2_hi[:, e, c, :], hid_lo[n % 2][:, c, :], start=False, stop=False)
                    last = nc.tensor.matmul(y[:, :], w2_lo[:, e, c, :], hid_hi[n % 2][:, c, :], start=False, stop=(c == FC - 1))
                last.then_inc(pe_y, 1)

            def finish(k, pb):
                pe.wait_ge(dve_fin, pb * ROWS + k + 1)
                for t in range(TILES):
                    tok = slice(t * P, (t + 1) * P)
                    last = nc.tensor.transpose(ps[6][:, tok], fin[k][:, tok], ident[:, :])
                last.then_inc(pe_fin, 1)

            def body(pb, r, q, first, last):
                opening = first and not there(pb - 1)
                for n in range(UNITS):
                    if opening and n == 0:
                        pe.wait_ge(act_att, B * H)
                    if n % E == 0:
                        gate(n, pb, r, q, first)
                    if first and n == 2 and there(pb - 1):
                        pe.wait_ge(act_cwT, q * ROWS + 1)
                        finish(1, pb - 1)
                    if last and n == 7:
                        pe.wait_ge(act_cwT, q * ROWS + 2)
                        finish(0, pb)
                    hidden(n, q)
                    if opening and n == 1:
                        project(B - 1, PAIRS - 1)
                    if opening and n == 2:
                        turn_gated(B - 1)
                    if n:
                        expert(n - 1, q)
                    if opening and n == 4:
                        turn_normal("h2", B - 1, ps[7])
                expert(UNITS - 1, q)

            pe.wait_ge(ld_ffn, 16 * (3 + TILES))
            loops(pe, body)
            pe.wait_ge(dve_res, B - 1)
            finish(1, PAIRED - 1)

        @block.scalar
        def _(act):
            act.dma_start(wmod_raw, wmod_d).then_inc(ld_wmod, 16)
            act.wait_ge(ld_c, 16)
            nc.scalar.activation(c_tanh, c_sb, ACT.Tanh, scale=0.5).then_inc(su_tanh, 1)

            def split(name):
                act.wait_ge(ld_w[name], 16)
                nc.scalar.copy(w_hi[name][:, :], raw[name]).then_inc(su_whi, 1)

            split("wq")
            split("wk")

            def item(b, n, kind, index, row):
                bank = bank_of(n)
                if kind in ("q", "k"):
                    act.wait_ge(pe_item[kind], nth(kind, index, row))
                    hi, col = (q_hi, QB) if kind == "q" else (k_hi, KB)
                    nc.scalar.activation(hi[index % 2][:, :], bank[:, :], ACT.Identity,
                                         bias=biasT[:, col + index:col + index + 1]).then_inc(act_item[kind], 1)
                if kind == "v" and index not in DVE_V:
                    half, t = divmod(index, TILES)
                    act.wait_ge(pe_item["v"], nth("v", index, row))
                    nc.scalar.copy(v_hl[half][:, t, :, 0:DH],
                                   bank[:, :].rearrange("p (h d) -> p h d", d=DH)).then_inc(act_item["v"], 1)
                if kind == "h":
                    act.wait_ge(dve_item["h"], row + 1)
                    nc.scalar.copy(h_hi[:, :], h_f[:, :]).then_inc(act_item["h"], 1)

            def exps(b, u, i):
                after(act, dve_min, (b * H + u) * TILES + i + 1)
                if isinstance(b, int) and b == 0 and u < 4 and i == 0:
                    act.wait_ge(dve_wlo if u < 2 else pool_wlo, u % 2 + 1)
                w = slice(P_OFF[i], P_OFF[i + 1])
                nc.scalar.activation(prob[:, u % 4, w], neg_s[:, w], ACT.Exp, scale=-1.0,
                                     bias=negmax[:, i:i + 1], accum_out=sums[:, u % 4, i:i + 1]).then_inc(act_exp, 1)

            def attended(b, u):
                pair, r = u // 2, DH * (u % 2)
                after(act, pe_pv, b * H + u + 1)
                if u % 2 == 0:
                    after(act, pool_alo, b * PAIRS + pair - 1)
                nc.scalar.activation(att[pair % 2][r:r + DH, :], ps[6][0:DH, :], ACT.Identity, bias=vbT[:, u:u + 1])
                nc.scalar.copy(att_of_lo[pair % 2][r:r + DH, :], ps[6][DH:P, :]).then_inc(act_att, 1)

            def turned(b, u, c):
                after(act, pe_t, (b * H + u) * 3 + c + 1)
                dst, width = CHUNKS[c][1], len(CHUNKS[c][0]) * P
                nc.scalar.copy(pt_hi[u % 2][:, dst:dst + width],
                               ps[4 + (u * 3 + c) % 2][:, 0:width]).then_inc(act_pt, 1)

            def step(b, u):
                todo = items(b, u)
                for part, i in ORDER["act"][u % 2]:
                    if part == "scores" and there(scored(b, u)[0]):
                        exps(*scored(b, u), i)
                    if part == "turn" and there(b):
                        turned(b, u, i)
                    if part == "values" and there(weighted(b, u)[0]):
                        attended(*weighted(b, u))
                    if part == "items":
                        for what in (todo[1:] if i else todo[:1]):
                            item(b, *what)

            for u in range(8, H_STEP + 1):
                step(-1, u)
            split("wv")
            split("wo")
            act.wait_ge(su_dve, 7)
            for u in range(H_STEP + 1, H):
                step(-1, u)
            for u in range(H):
                step(0, u)
            with act.Fori(1, B - 1) as b:
                for u in range(H):
                    step(b, u)
            for u in range(H):
                step(B - 1, u)
            step(B, 0)

            def gelus(n, q):
                e = n % E
                for c in range(FC):
                    g = q * (UNITS * FC) + n * FC + c
                    act.wait_ge(pe_hid, g + 1)
                    b1 = B1 + e * FC + c
                    nc.scalar.activation(hid[n % 2][:, c, :], ps[c][:, :], ACT.Gelu_apprx_tanh,
                                         bias=biasT[:, b1:b1 + 1]).then_inc(act_hid, 1)
                    if e == 0 and c == 2:
                        act.wait_ge(dve_gate, (q * ROWS + n // E) * GATE + 10)
                        nc.scalar.activation(th[:, :, :], gap[:, :, :], ACT.Tanh).then_inc(act_tanh, 1)
                    if e == 1 and c == 2:
                        copy_weights(n, q)

            def highs(n, q):
                for c in (0, 1):
                    act.wait_ge(act_hid, q * (UNITS * FC) + n * FC + c + 1)
                    nc.scalar.copy(hid_hi[n % 2][:, c, :], hid[n % 2][:, c, :]).then_inc(act_hi, 1)

            def copy_weights(n, q):
                act.wait_ge(pe_cwT, q * ROWS + n // E + 1)
                nc.scalar.activation(cwT[n // E][:, :], ps[6][0:E, :], ACT.Identity, scale=0.5).then_inc(act_cwT, 1)

            def load(k, pb):
                if there(pb - 1):
                    act.wait_ge(dve_fin, (pb - 1) * ROWS + k + 1)
                else:
                    act.wait_ge(dve_item["h2"], k + 1)
                nc.scalar.copy(cur[k][:, :], cur_all[:, bass.ds((pb * ROWS + k) * S, S)]).then_inc(act_cur, 1)

            def body(pb, r, q, first, last):
                for n in range(UNITS):
                    if first and n == 2 and there(pb - 1):
                        load(1, pb)
                    if last and n == 7 and not isinstance(pb, int):
                        load(0, pb + 1)
                    gelus(n, q)
                    highs(n, q)

            load(0, 0)
            nc.scalar.copy(cur_hi[0][:, :], cur_all[:, 0:S]).then_inc(act_chi, 1)
            act.wait_ge(ld_ffn, 16 * (3 + TILES))
            for e in ACT_SPLITS:
                nc.scalar.copy(w1_hi[:, e, :], w1_raw[:, e * F:(e + 1) * F]).then_inc(ffn_act_whi, 1)
            for e in ACT_SPLITS:
                w = slice(e * FC * D, (e + 1) * FC * D)
                nc.scalar.copy(w2_hi[:, e, :, :], w2_raw[:, w].rearrange("p (c d) -> p c d", d=D)).then_inc(ffn_act_whi, 1)
            load(1, 0)
            loops(act, body)

        @block.vector
        def _(dve):
            dve.wait_ge(su_tanh, 1)
            nc.vector.scalar_tensor_tensor(out=c_act, in0=c_tanh, scalar=1.0, in1=c_sb, op0=ALU.add, op1=ALU.mult).then_inc(su_dve, 1)

            def item(b, n, kind, index, row):
                bank = bank_of(n)
                if kind in ("q", "k"):
                    hi, lo, col = (q_hi, q_lo, QB) if kind == "q" else (k_hi, k_lo, KB)
                    dve.wait_ge(act_item[kind], nth(kind, index, row))
                    nc.vector.scalar_tensor_tensor(out=lo[index % 2][:, :], in0=bank[:, :], scalar=biasT[:, col + index:col + index + 1],
                                                   in1=hi[index % 2][:, :].bitcast(F32), op0=ALU.add, op1=ALU.subtract).then_inc(dve_item[kind], 1)
                if kind == "v":
                    half, t = divmod(index, TILES)
                    if index in DVE_V:
                        dve.wait_ge(pe_item["v"], nth("v", index, row))
                        nc.vector.tensor_copy(v_hl[half][:, t, :, 0:DH],
                                              bank[:, :].rearrange("p (h d) -> p h d", d=DH)).then_inc(dve_vhi, 1)
                        dve.wait_ge(dve_vhi, row * len(DVE_V) + DVE_V.index(index) + 1)
                    else:
                        dve.wait_ge(act_item["v"], row * (2 * TILES - len(DVE_V)) + len([i for i in range(index + 1) if i not in DVE_V]))
                    nc.vector.tensor_tensor(v_hl[half][:, t, :, DH:2 * DH], bank[:, :].rearrange("p (h d) -> p h d", d=DH),
                                            v_hl[half][:, t, :, 0:DH].bitcast(F32), ALU.subtract).then_inc(dve_item["v"], 1)
                if kind == "h":
                    dve.wait_ge(pe_item["h"], row + 1)
                    after(dve, pool_hlo, row)
                    nc.vector.tensor_scalar(h_f[:, :], bank[:, :], modT[:, 1, bass.ds(row, 1)], modT[:, 0, bass.ds(row, 1)],
                                            ALU.mult, ALU.add).then_inc(dve_item["h"], 1)
                if kind == "h2":
                    modulate2(row, bank)

            def minima(b, u, i):
                after(dve, act_exp, (b * H + u - 1) * TILES + i + 1)
                after(dve, pe_s, (b * H + u) * TILES + i + 1)
                dve.sem_inc(dve_waited, 1)
                w = (i + 1) * P
                nc.vector.tensor_tensor_reduce(neg_s[:, P_OFF[i]:P_OFF[i + 1]], ps[2 + i % 2][:, 0:w], mask[:, S - w:S],
                                               -SCALE, BIG, ALU.add, ALU.min, negmax[:, i:i + 1]).then_inc(dve_min, 1)

            def turned(b, u, c):
                after(dve, act_pt, (b * H + u) * 3 + c + 1)
                dst, width = CHUNKS[c][1], len(CHUNKS[c][0]) * P
                nc.vector.tensor_tensor(pt_lo[u % 2][:, dst:dst + width], ps[4 + (u * 3 + c) % 2][:, 0:width],
                                        pt_hi[u % 2][:, dst:dst + width].bitcast(F32), ALU.subtract).then_inc(dve_pt, 1)

            def inverse(b, u):
                after(dve, act_exp, (b * H + u + 1) * TILES)
                nc.vector.reciprocal(rinv[:, u % 4, :], sums[:, u % 4, :]).then_inc(dve_rinv, 1)

            def moments(row, stats, mv, ve, s_bn, s_ve):
                dve.sem_inc(dve_waited, 1)
                for t in range(TILES):
                    last = nc.vector.bn_stats(stats[:, t, :], x_sb[:, bass.ds(row * S + t * D, D)])
                last.then_inc(s_bn, 1)
                after(dve, s_bn, row * 2 + 1)
                dve.sem_inc(dve_waited, 1)
                for t in range(TILES):
                    last = nc.vector.bn_aggr(mv[:, t, :], stats[:, t, :])
                last.then_inc(s_bn, 1)
                after(dve, s_bn, row * 2 + 2)
                nc.vector.tensor_scalar(ve[:, :], mv[:, :, 1], EPS, None, ALU.add).then_inc(s_ve, 1)

            def normalise(row, norm, mv, rstd, s_rstd, s_norm):
                after(dve, s_rstd, row + 1)
                for t in range(TILES):
                    last = nc.vector.tensor_scalar(norm[:, t * D:(t + 1) * D], x_sb[:, bass.ds(row * S + t * D, D)],
                                                   mv[:, t, 0:1], rstd[:, t:t + 1], ALU.subtract, ALU.mult)
                last.then_inc(s_norm, 1)

            def gate_attention(row):
                after(dve, pe_o, (row + 1) * PAIRS)
                nc.vector.tensor_scalar(gated[:, :], ps[7][:, :], biasT[:, OB:OB + 1], modT[:, 2, bass.ds(row, 1)],
                                        ALU.add, ALU.mult).then_inc(dve_y, 1)

            def add_attention(row):
                after(dve, pe_yt, row + 1)
                xr = x_sb[:, bass.ds(row * S, S)]
                nc.vector.tensor_tensor(xr, ps[7][:, :], xr, ALU.add).then_inc(dve_x1, 1)

            def modulate2(row, bank):
                after(dve, pe_item["h2"], row + 1)
                nc.vector.tensor_scalar(cur_all[:, bass.ds(row * S, S)], bank[:, :], modT[:, 4, bass.ds(row, 1)],
                                        modT[:, 3, bass.ds(row, 1)], ALU.mult, ALU.add).then_inc(dve_item["h2"], 1)

            def step(b, u):
                if u == AT["gate"] and there(b - 1):
                    gate_attention(b - 1)
                todo = items(b, u)
                if u == AT["add"] and there(b - 1):
                    add_attention(b - 1)
                for part, i in ORDER["dve"][u % 2]:
                    if part == "scores" and there(scored(b, u)[0]):
                        minima(*scored(b, u), i)
                    if part == "turn" and there(b):
                        turned(b, u, i)
                    if part == "items":
                        for what in (todo[1:] if i else todo[:1]):
                            item(b, *what)
                    if part == "inverse" and there(scored_before(b, u)[0]):
                        inverse(*scored_before(b, u))
                if u == AT["moments2"] and there(b - 1):
                    after(dve, dve_x1, b)
                    moments(b - 1, bn2, mv2, ve2, dve_bn2, dve_ve2)
                if u == AT["normal2"] and there(b - 1):
                    normalise(b - 1, norm2, mv2, rstd2, pool_rstd2, dve_norm2)
                if u == AT["moments1"] and there(b + 1):
                    moments(b + 1, bn1, mv1, ve1, dve_bn1, dve_ve1)
                if u == AT["normal1"] and there(b + 1):
                    normalise(b + 1, norm1, mv1, rstd1, pool_rstd1, dve_norm1)

            dve.wait_ge(su_pe, 1)
            nc.vector.tensor_scalar(siluT, ps[2][:, 128:128 + B], 0.5, None, ALU.mult).then_inc(su_dve, 1)
            dve.wait_ge(ld_x[0], 16)
            for u in range(8, AT["normal1"] + 1):
                step(-1, u)
            dve.wait_ge(su_pe, 2)
            nc.vector.tensor_copy(modT[:, :, :], ps[3][:, 0:6 * B].rearrange("p (j b) -> p j b", b=B)).then_inc(su_dve, 1)
            dve.wait_ge(su_dve, 3)
            g = modT[:, 2:6:3, :]
            ga_pos_v = ga_pos.rearrange("p (j b) -> p j b", b=B)
            ga_neg_v = ga_neg.rearrange("p (j b) -> p j b", b=B)
            nc.vector.tensor_scalar(ga_pos_v, g, 0.0, 2.0, ALU.is_ge, ALU.mult)
            nc.vector.tensor_scalar(ga_neg_v, g, -1.0, None, ALU.mult)
            nc.vector.tensor_scalar(modT[:, 1:5:3, :], modT[:, 1:5:3, :], 1.0, None, ALU.add).then_inc(su_dve, 1)
            dve.wait_ge(su_dve, 4)
            nc.vector.tensor_scalar(ga_pos_v, ga_pos_v, 1.0, None, ALU.subtract)
            nc.vector.tensor_tensor(ga_neg_v, ga_neg_v, g, ALU.max).then_inc(su_dve, 1)
            dve.wait_ge(su_dve, 5)
            nc.vector.scalar_tensor_tensor(out=g, in0=ga_neg_v, scalar=0.25, in1=ga_pos_v, op0=ALU.max, op1=ALU.mult).then_inc(su_dve, 1)
            dve.wait_ge(su_dve, 6)
            for u in range(AT["normal1"] + 1, H_STEP + 1):
                step(-1, u)
            for n, name in enumerate(("wq", "wk")):
                dve.wait_ge(su_whi, n + 1)
                nc.vector.tensor_tensor(w_lo[name][:, :], raw[name], w_hi[name][:, :].bitcast(F32), ALU.subtract).then_inc(dve_wlo, 1)
            dve.wait_ge(su_pe, 3)
            nc.vector.tensor_copy(biasT[:, 0:NROWS], ps[2][:, 0:NROWS])
            nc.vector.tensor_copy(vbT[:, :], ps[2][0:DH, 64:64 + H]).then_inc(su_dve, 1)
            dve.wait_ge(su_const, 7)
            for u in range(H_STEP + 1, H):
                step(-1, u)
            dve.wait_ge(ld_x[1], 16)
            for u in range(H):
                step(0, u)
            with dve.Fori(1, B - 1) as b:
                for u in range(H):
                    step(b, u)
            for u in range(H):
                step(B - 1, u)
            step(B, 0)

            def gates(n, r, q):
                base = (q * ROWS + n // E) * GATE
                by_j = logit[:, :, :].unsqueeze(2).to_broadcast([P, TILES, E, E])
                by_e = logit[:, :, :].unsqueeze(3).to_broadcast([P, TILES, E, E])
                dve.wait_ge(pe_gate, q * ROWS + n // E + 1)
                nc.vector.tensor_tensor(logit[:, :, :], ps[6][:, 0:TILES * E].rearrange("p (t e) -> p t e", e=E),
                                        bg_sb[:, bass.ds(r, 1), :, :].rearrange("p r t e -> p (r t) e"), ALU.add).then_inc(dve_gate, 1)
                dve.wait_ge(dve_gate, base + 1)
                nc.vector.tensor_tensor(gt[:, :, :, :], by_j, by_e, ALU.is_gt).then_inc(dve_gate, 1)
                nc.vector.tensor_tensor(eq[:, :, :, :], by_j, by_e, ALU.is_equal).then_inc(dve_gate, 1)
                dve.wait_ge(dve_gate, base + 3)
                nc.vector.tensor_tensor(eq[:, :, :, :], eq[:, :, :, :],
                                        earlier[:, :, :].unsqueeze(1).to_broadcast([P, TILES, E, E]), ALU.mult).then_inc(dve_gate, 1)
                dve.wait_ge(dve_gate, base + 4)
                nc.vector.tensor_tensor(gt[:, :, :, :], gt[:, :, :, :], eq[:, :, :, :], ALU.add).then_inc(dve_gate, 1)
                dve.wait_ge(dve_gate, base + 5)
                nc.vector.tensor_reduce(rank[:, :, :], gt[:, :, :, :], AX_X, ALU.add).then_inc(dve_gate, 1)
                dve.wait_ge(dve_gate, base + 6)
                nc.vector.tensor_scalar(chosen[:, :, :], rank[:, :, :], 2.0, None, ALU.is_lt).then_inc(dve_gate, 1)
                dve.wait_ge(dve_gate, base + 7)
                nc.vector.tensor_tensor(picked[:, :, :], logit[:, :, :], chosen[:, :, :], ALU.mult).then_inc(dve_gate, 1)
                dve.wait_ge(dve_gate, base + 8)
                nc.vector.tensor_reduce(pair_sum[:, :], picked[:, :, :], AX_X, ALU.add).then_inc(dve_gate, 1)
                dve.wait_ge(dve_gate, base + 9)
                nc.vector.scalar_tensor_tensor(out=gap[:, :, :], in0=pair_sum[:, :].unsqueeze(2).to_broadcast([P, TILES, E]),
                                               scalar=-0.5, in1=logit[:, :, :], op0=ALU.mult, op1=ALU.add).then_inc(dve_gate, 1)

            def weights(n, q):
                base = (q * ROWS + n // E) * GATE
                dve.wait_ge(act_tanh, q * ROWS + n // E + 1)
                nc.vector.scalar_tensor_tensor(out=cw2[:, :, :], in0=th[:, :, :], scalar=1.0, in1=chosen[:, :, :],
                                               op0=ALU.add, op1=ALU.mult).then_inc(dve_gate, 1)

            def lows(n, q):
                base = q * (UNITS * FC) + n * FC
                for part, c in (("lo", 0), ("hi", 2), ("lo", 1), ("hi", 3), ("lo", 2), ("lo", 3)):
                    if part == "hi":
                        dve.wait_ge(act_hid, base + c + 1)
                        nc.vector.tensor_copy(hid_hi[n % 2][:, c, :], hid[n % 2][:, c, :]).then_inc(dve_hi, 1)
                        continue
                    if c < 2:
                        dve.wait_ge(act_hi, q * (UNITS * 2) + n * 2 + c + 1)
                    else:
                        dve.wait_ge(dve_hi, (q * UNITS + n) * 2 + c - 1)
                    nc.vector.tensor_tensor(hid_lo[n % 2][:, c, :], hid[n % 2][:, c, :], hid_hi[n % 2][:, c, :].bitcast(F32),
                                            ALU.subtract).then_inc(dve_lo, 1)

            def shares(n, q):
                e = n % E
                dve.wait_ge(pe_y, q * UNITS + n + 1)
                dve.wait_ge(cw_in[n // E][e], q * 16 + 16)
                after(dve, pool_cur, q * UNITS + n - 1)
                nc.vector.scalar_tensor_tensor(out=share[n % 2][:, :], in0=ps[4 + n % 2][:, :], scalar=biasT[:, B2 + e:B2 + e + 1],
                                               in1=cwb[n // E][:, e, :], op0=ALU.add, op1=ALU.mult).then_inc(dve_share, 1)

            def finish(k, pb):
                dve.wait_ge(pool_cur, (pb * R + R - 1) * UNITS + (k + 1) * E)
                nc.vector.tensor_scalar(fin[k][:, :], cur[k][:, :], modT[:, 5, bass.ds(pb * ROWS + k, 1)], None,
                                        ALU.mult).then_inc(dve_fin, 1)

            def result(k, pb):
                dve.wait_ge(pe_fin, pb * ROWS + k + 1)
                xr = x_sb[:, bass.ds((pb * ROWS + k) * S, S)]
                nc.vector.tensor_tensor(xr, ps[6][:, :], xr, ALU.add).then_inc(dve_res, 1)

            def body(pb, r, q, first, last):
                opening = first and not there(pb - 1)
                for n in range(UNITS):
                    if n % E == 0:
                        gates(n, r, q)
                        if opening and n == 0:
                            split_second_weights()
                        weights(n, q)
                    lows(n, q)
                    if first and n == 0 and there(pb - 1):
                        finish(1, pb - 1)
                    if opening and n == 1:
                        gate_attention(B - 1)
                    for m in SHARES[n]:
                        shares(m, q)
                    if opening and n == 2:
                        add_attention(B - 1)
                        after(dve, dve_x1, B)
                        moments(B - 1, bn2, mv2, ve2, dve_bn2, dve_ve2)
                    if opening and n == 3:
                        normalise(B - 1, norm2, mv2, rstd2, pool_rstd2, dve_norm2)
                    if opening and n == 5:
                        modulate2(B - 1, ps[7])
                    if first and n == 2 and there(pb - 1):
                        result(1, pb - 1)
                    if last:
                        if n == 5:
                            finish(0, pb)
                        if n == 7:
                            result(0, pb)
                shares(UNITS - 1, q)

            dve.wait_ge(pe_pv, B * H)
            dve.wait_ge(act_chi, 1)
            nc.vector.tensor_tensor(cur_lo[0][:, :], cur_all[:, 0:S], cur_hi[0][:, :].bitcast(F32), ALU.subtract).then_inc(dve_clo, 1)
            for i, e in enumerate(ACT_SPLITS):
                dve.wait_ge(ffn_act_whi, i + 1)
                nc.vector.tensor_tensor(w1_lo[:, e, :], w1_raw[:, e * F:(e + 1) * F], w1_hi[:, e, :].bitcast(F32),
                                        ALU.subtract).then_inc(ffn_dve_wlo, 1)

            def split_second_weights():
                for i, e in enumerate(ACT_SPLITS):
                    dve.wait_ge(ffn_act_whi, len(ACT_SPLITS) + i + 1)
                    w = slice(e * FC * D, (e + 1) * FC * D)
                    nc.vector.tensor_tensor(w2_lo[:, e, :, :], w2_raw[:, w].rearrange("p (c d) -> p c d", d=D),
                                            w2_hi[:, e, :, :].bitcast(F32), ALU.subtract).then_inc(ffn_dve_wlo, 1)

            dve.wait_ge(ld_ffn, 16 * (3 + TILES))
            dve.wait_ge(f_const, 2)
            loops(dve, body)
            finish(1, PAIRED - 1)
            result(1, PAIRED - 1)

        @block.gpsimd
        def _(pool):
            nc.gpsimd.memset(ident[:, :], 0.0).then_inc(su_const, 1)
            nc.gpsimd.memset(mask[:, :], 0.0).then_inc(su_const, 1)
            nc.gpsimd.memset(minus_half[:, :], -0.5).then_inc(su_const, 1)
            pool.wait_ge(su_const, 3)
            nc.gpsimd.affine_select(out=ident[:, :], in_=ident[:, :], compare_op=ALU.not_equal, fill=1.0, base=0,
                                    pattern=[[-1, P]], channel_multiplier=1).then_inc(su_const, 1)
            tri = mask[:, S - P:S]
            nc.gpsimd.affine_select(out=tri, in_=tri, compare_op=ALU.is_ge, fill=NEG, base=0,
                                    pattern=[[-1, P]], channel_multiplier=1).then_inc(su_const, 1)
            for part in (pt_hi, pt_lo):
                for i in range(2):
                    last = nc.gpsimd.memset(part[i][:, PT_OFF[3]:PT_DATA3].bitcast(F32), 0.0)
                last.then_inc(su_const, 1)

            nc.gpsimd.memset(earlier[:, :, :], 1.0).then_inc(f_const, 1)
            pool.wait_ge(f_const, 1)
            nc.gpsimd.affine_select(out=earlier[:, :, :], in_=earlier[:, :, :], compare_op=ALU.is_gt, fill=0.0, base=0,
                                    pattern=[[1, E], [-1, E]], channel_multiplier=0).then_inc(f_const, 1)

            def root2(row):
                after(pool, dve_ve2, row + 1)
                nc.gpsimd.tensor_tensor(rstd2[:, :], ve2[:, :], minus_half[:, :], ALU.pow).then_inc(pool_rstd2, 1)

            def step(b, u):
                if u == H_STEP and there(b + 1):
                    pool.wait_ge(act_item["h"], b + 2)
                    nc.gpsimd.tensor_tensor(h_lo[:, :], h_f[:, :], h_hi[:, :].bitcast(F32), ALU.subtract).then_inc(pool_hlo, 1)
                row, head = weighted(b, u)
                if there(row) and head % 2 == 1:
                    pair = head // 2
                    after(pool, act_att, row * H + head + 1)
                    nc.gpsimd.tensor_tensor(att[pair % 2][:, :], att[pair % 2][:, :], att_of_lo[pair % 2][:, :],
                                            ALU.add).then_inc(pool_att, 1)
                    after(pool, pool_att, row * PAIRS + pair + 1)
                    pool.sem_inc(pool_waited, 1)
                    nc.gpsimd.tensor_scalar(att_hi[pair % 2][:, :], att[pair % 2][:, :], 1.0, 1.0, ALU.mult, ALU.mult).then_inc(pool_ahi, 1)
                    after(pool, pool_ahi, row * PAIRS + pair + 1)
                    nc.gpsimd.tensor_tensor(att_lo[pair % 2][:, :], att[pair % 2][:, :], att_hi[pair % 2][:, :].bitcast(F32),
                                            ALU.subtract).then_inc(pool_alo, 1)
                if u == AT["root2"] and there(b - 1):
                    root2(b - 1)
                if u == AT["root1"] and there(b + 1):
                    after(pool, dve_ve1, b + 2)
                    nc.gpsimd.tensor_tensor(rstd1[:, :], ve1[:, :], minus_half[:, :], ALU.pow).then_inc(pool_rstd1, 1)
                row, head = scored(b, u)
                if there(row):
                    after(pool, dve_rinv, row * H + head + 1)
                    pool.sem_inc(pool_waited, 1)
                    for i in range(TILES):
                        w = slice(P_OFF[i], P_OFF[i + 1])
                        last = nc.gpsimd.tensor_scalar(prob[:, head % 4, w], prob[:, head % 4, w], rinv[:, head % 4, i:i + 1], 1.0,
                                                       ALU.mult, ALU.mult)
                    last.then_inc(pool_prob, 1)

            for u in range(8, H_STEP + 1):
                step(-1, u)
            for n, name in enumerate(("wv", "wo")):
                pool.wait_ge(su_whi, n + 3)
                nc.gpsimd.tensor_tensor(w_lo[name][:, :], raw[name], w_hi[name][:, :].bitcast(F32), ALU.subtract).then_inc(pool_wlo, 1)
            for u in range(H_STEP + 1, H):
                step(-1, u)
            for u in range(H):
                step(0, u)
            with pool.Fori(1, B - 1) as b:
                for u in range(H):
                    step(b, u)
            for u in range(H):
                step(B - 1, u)
            step(B, 0)

            def split(k, q):
                pool.sem_inc(pool_waited, 1)
                nc.gpsimd.tensor_scalar(cur_hi[k][:, :], cur[k][:, :], 1.0, 1.0, ALU.mult, ALU.mult).then_inc(pool_chi, 1)
                pool.wait_ge(pool_chi, q * ROWS + k)
                nc.gpsimd.tensor_tensor(cur_lo[k][:, :], cur[k][:, :], cur_hi[k][:, :].bitcast(F32), ALU.subtract).then_inc(pool_clo, 1)

            def add(n, pb, q, last):
                k, e = divmod(n, E)
                pool.wait_ge(dve_share, q * UNITS + n + 1)
                after(pool, pool_cur, q * UNITS + n)
                nc.gpsimd.tensor_tensor(cur[k][:, :], cur[k][:, :], share[n % 2][:, :], ALU.add).then_inc(pool_cur, 1)
                if e == E - 1 and not last:
                    pool.wait_ge(pool_cur, q * UNITS + n + 1)
                    split(k, q + 1)

            def split_new(k, pb):
                pool.wait_ge(act_cur, pb * ROWS + k + 1)
                split(k, pb * R)

            def body(pb, r, q, first, last):
                for n in range(UNITS):
                    if first and n == 0 and there(pb - 1):
                        split_new(1, pb)
                    add(n, pb, q, last)
                    if first and n == 1 and not there(pb - 1):
                        root2(B - 1)
                    if last and n == 5 and not isinstance(pb, int):
                        split_new(0, pb + 1)

            def split_weights(raw, hi, lo, count):
                nc.gpsimd.tensor_scalar(hi, raw, 1.0, 1.0, ALU.mult, ALU.mult).then_inc(ffn_pool_whi, 1)
                pool.wait_ge(ffn_pool_whi, count)
                nc.gpsimd.tensor_tensor(lo, raw, hi.bitcast(F32), ALU.subtract).then_inc(ffn_pool_wlo, 1)

            split_new(1, 0)
            pool.wait_ge(ld_ffn, 16 * (3 + TILES))
            for i, e in enumerate(POOL_SPLITS):
                w = slice(e * F, (e + 1) * F)
                split_weights(w1_raw[:, w], w1_hi[:, e, :], w1_lo[:, e, :], 2 * i + 1)
                split_weights(w2_raw[:, w], w2_hi[:, e, :, :].rearrange("p c d -> p (c d)"),
                              w2_lo[:, e, :, :].rearrange("p c d -> p (c d)"), 2 * i + 2)
            loops(pool, body)


_INS = ["L0_attn_x", "L0_attn_Q_w", "L0_attn_Q_b", "L0_attn_K_w", "L0_attn_K_b", "L0_attn_V_w", "L0_attn_V_b", "L0_attn_O_w",
        "L0_attn_O_b", "L0_ffn_Wg", "L0_ffn_bg", "L0_ffn_W1", "L0_ffn_b1", "L0_ffn_W2", "L0_ffn_b2", "L0_c", "L0_wmod"]


def kernel(**inputs):
    import numpy as np
    import concourse.bacc as bacc
    from concourse.bass_utils import run_bass_kernel_spmd

    nc = bacc.Bacc("TRN2", target_bir_lowering=False, num_devices=1)
    arrays, args = {}, []
    for name in _INS:
        a = np.ascontiguousarray(inputs[name])
        arrays["in_" + name] = a
        args.append(nc.dram_tensor("in_" + name, a.shape, mybir.dt.from_np(a.dtype), kind="ExternalInput").ap())
    out = nc.dram_tensor("out_x", inputs["L0_attn_x"].shape, F32, kind="ExternalOutput").ap()
    adaln_block(nc, args, out)
    r = run_bass_kernel_spmd(nc, [arrays], core_ids=[0])
    return r.results[0]["out_x"]
```
